# Optimizing a Trainium2 kernel written in Bass

```python
import numpy as np
import jax
import jax.numpy as jnp

def _softmax(x, axis=-1):
    return jax.nn.softmax(x, axis=axis)

def _gelu(x):
    return jax.nn.gelu(x, approximate=True)

def _silu(x):
    return jax.nn.silu(x)

def _sigmoid(x):
    return jax.nn.sigmoid(x)

def _layernorm(x, axis=-1, eps=1e-05):
    m = jnp.mean(x, axis=axis, keepdims=True)
    v = jnp.var(x, axis=axis, keepdims=True)
    return (x - m) / jnp.sqrt(v + eps)

def _scatter_add(tgt, idx, src, axis=0):
    return tgt.at[idx].add(src)

def _segment_sum(src, seg, n):
    return jax.ops.segment_sum(src, seg, n)
kernel_name = 'mk_vit_tower_postln_d1_tok_img256_r4_6442ec'

def setup_inputs(seed: int=0):
    np.random.seed(seed)
    _w = jnp.asarray

    def _rec_inputs():
        import jax
        import jax.numpy as jnp
        _rk = jax.random.key(seed)
        x = -0.000395706 + 0.999959 * jax.random.normal(jax.random.fold_in(_rk, 1), (32, 1, 224, 224), jnp.float32)
        return x
    x = _rec_inputs()

    def _L0_tok_setup():
        import jax, jax.numpy as jnp
        import numpy as np
        IMAGE_SIZE = 224
        PATCH_SIZE = 7
        EMBED_DIM = 64
        NUM_PATCHES = (IMAGE_SIZE // PATCH_SIZE) ** 2
        PATCH_DIM = PATCH_SIZE ** 2
        key = jax.random.key(seed)
        kx, kw, kb, kp = jax.random.split(key, 4)
        x = jax.random.normal(kx, (64, 1, IMAGE_SIZE, IMAGE_SIZE), dtype=jnp.float32)
        bound = 1.0 / np.sqrt(PATCH_DIM)
        W = jax.random.uniform(kw, (EMBED_DIM, PATCH_DIM), minval=-bound, maxval=bound, dtype=jnp.float32)
        b = jax.random.uniform(kb, (EMBED_DIM,), minval=-bound, maxval=bound, dtype=jnp.float32)
        pos = jax.random.uniform(kp, (1, NUM_PATCHES, EMBED_DIM), dtype=jnp.float32)
        return {'x': x, 'W': W, 'b': b, 'pos': pos}
    _L0_tok_all = _L0_tok_setup()
    _L0_tok_in = {k: v for k, v in _L0_tok_all.items() if k in ('W', 'b', 'pos')}
    del _L0_tok_all

    def _L0_attn_setup():
        import jax, jax.numpy as jnp
        import numpy as np
        import math
        B, S, D = (4, 1024, 64)
        key = jax.random.key(seed)
        ks = jax.random.split(key, 9)
        s = 1.0 / math.sqrt(D)
        return {'src': jax.random.normal(ks[0], (B, S, D), dtype=jnp.float32), 'Wq': jax.random.normal(ks[1], (D, D), dtype=jnp.float32) * s, 'bq': jax.random.normal(ks[2], (D,), dtype=jnp.float32) * s, 'Wk': jax.random.normal(ks[3], (D, D), dtype=jnp.float32) * s, 'bk': jax.random.normal(ks[4], (D,), dtype=jnp.float32) * s, 'Wv': jax.random.normal(ks[5], (D, D), dtype=jnp.float32) * s, 'bv': jax.random.normal(ks[6], (D,), dtype=jnp.float32) * s, 'Wo': jax.random.normal(ks[7], (D, D), dtype=jnp.float32) * s, 'bo': jax.random.normal(ks[8], (D,), dtype=jnp.float32) * s}
    _L0_attn_all = _L0_attn_setup()
    _L0_attn_in = {k: v for k, v in _L0_attn_all.items() if k in ('Wq', 'bq', 'Wk', 'bk', 'Wv', 'bv', 'Wo', 'bo')}
    del _L0_attn_all

    def _L0_ffn_setup():
        import math
        import jax, jax.numpy as jnp
        import numpy as np
        CAPACITY_FACTOR = 1.25
        key = jax.random.key(seed)
        ks = jax.random.split(key, 5)
        B, L, D, F, E = (8, 2048, 64, 256, 8)
        h = jax.random.normal(ks[0], (B, L, D), dtype=jnp.float32)
        gate_w = jax.random.normal(ks[1], (D, E), dtype=jnp.float32) * 0.02
        gate_b = jnp.zeros((E,), dtype=jnp.float32)
        w1 = jax.random.normal(ks[2], (E, D, F), dtype=jnp.float32) * (1.0 / math.sqrt(D))
        b1 = jnp.zeros((E, F), dtype=jnp.float32)
        w2 = jax.random.normal(ks[3], (E, F, D), dtype=jnp.float32) * (1.0 / math.sqrt(F))
        b2 = jnp.zeros((E, D), dtype=jnp.float32)
        return {'h': h, 'gate_w': gate_w, 'gate_b': gate_b, 'w1': w1, 'b1': b1, 'w2': w2, 'b2': b2}
    _L0_ffn_all = _L0_ffn_setup()
    _L0_ffn_in = {k: v for k, v in _L0_ffn_all.items() if k in ('gate_w', 'gate_b', 'w1', 'b1', 'w2', 'b2')}
    del _L0_ffn_all
    return {'x': x, 'L0_tok_W': _L0_tok_in['W'], 'L0_tok_b': _L0_tok_in['b'], 'L0_tok_pos': _L0_tok_in['pos'], 'L0_attn_Wq': _L0_attn_in['Wq'], 'L0_attn_bq': _L0_attn_in['bq'], 'L0_attn_Wk': _L0_attn_in['Wk'], 'L0_attn_bk': _L0_attn_in['bk'], 'L0_attn_Wv': _L0_attn_in['Wv'], 'L0_attn_bv': _L0_attn_in['bv'], 'L0_attn_Wo': _L0_attn_in['Wo'], 'L0_attn_bo': _L0_attn_in['bo'], 'L0_ffn_gate_w': _L0_ffn_in['gate_w'], 'L0_ffn_gate_b': _L0_ffn_in['gate_b'], 'L0_ffn_w1': _L0_ffn_in['w1'], 'L0_ffn_b1': _L0_ffn_in['b1'], 'L0_ffn_w2': _L0_ffn_in['w2'], 'L0_ffn_b2': _L0_ffn_in['b2']}

def reference(x, L0_tok_W, L0_tok_b, L0_tok_pos, L0_attn_Wq, L0_attn_bq, L0_attn_Wk, L0_attn_bk, L0_attn_Wv, L0_attn_bv, L0_attn_Wo, L0_attn_bo, L0_ffn_gate_w, L0_ffn_gate_b, L0_ffn_w1, L0_ffn_b1, L0_ffn_w2, L0_ffn_b2):
    import jax
    import jax.numpy as jnp

    def _L0_tok_ref(x, W, b, pos):
        import jax, jax.numpy as jnp
        import numpy as np
        IMAGE_SIZE = 224
        PATCH_SIZE = 7
        EMBED_DIM = 64
        NUM_PATCHES = (IMAGE_SIZE // PATCH_SIZE) ** 2
        PATCH_DIM = PATCH_SIZE ** 2
        B = x.shape[0]
        p = PATCH_SIZE
        n = IMAGE_SIZE // p
        patches = x.reshape(B, n, p, n, p).transpose(0, 1, 3, 2, 4).reshape(B, n * n, p * p)
        out = jnp.einsum('bnd,ed->bne', patches, W) + b + pos
        return out

    def _L0_attn_ref(src, Wq, bq, Wk, bk, Wv, bv, Wo, bo):
        import jax, jax.numpy as jnp
        import numpy as np
        import math
        B, S, D = (4, 1024, 64)
        q = src @ Wq.T + bq
        k = src @ Wk.T + bk
        v = src @ Wv.T + bv
        row_mask = (q[:, :, 0] != 0) & (k[:, :, 0] != 0)
        mask = row_mask[:, :, None]
        scale = 1.0 / math.sqrt(D)
        scores = jnp.einsum('bid,bjd->bij', q, k) * scale
        scores = jnp.where(mask, scores, jnp.float32(-1000000000.0))
        prob = jax.nn.softmax(scores, axis=-1)
        prob = jnp.where(mask, prob, 0.0)
        out = jnp.einsum('bij,bjd->bid', prob, v)
        return out @ Wo.T + bo

    def _L0_ffn_ref(h, gate_w, gate_b, w1, b1, w2, b2):
        import math
        import jax, jax.numpy as jnp
        import numpy as np
        CAPACITY_FACTOR = 1.25
        B, L, D = h.shape
        E = gate_w.shape[1]
        T = B * L
        C = max(1, math.ceil(CAPACITY_FACTOR * T / E))
        x = h.reshape(T, D)
        logits = x @ gate_w + gate_b
        probs = jax.nn.softmax(logits, axis=-1)
        idx = jnp.argmax(probs, axis=-1)
        prb = jnp.take_along_axis(probs, idx[:, None], axis=1)[:, 0]
        one_hot = jax.nn.one_hot(idx, E, dtype=jnp.float32)
        pos = (jnp.cumsum(one_hot, axis=0) * one_hot).sum(-1).astype(jnp.int32) - 1
        kept = pos < C
        pos_safe = jnp.where(kept, pos, C)
        buf = jnp.zeros((E, C, D), dtype=h.dtype).at[idx, pos_safe].set(x, mode='drop')
        hmid = jax.nn.relu(jnp.einsum('ecd,edf->ecf', buf, w1) + b1[:, None, :])
        ybuf = jnp.einsum('ecf,efd->ecd', hmid, w2) + b2[:, None, :]
        pos_g = jnp.minimum(pos, C - 1)
        y_tok = ybuf[idx, pos_g] * (prb * kept)[:, None]
        y = y_tok.reshape(B, L, D)
        y = jnp.nan_to_num(y, nan=0.0, posinf=10000.0, neginf=-10000.0)
        return y
    h = _L0_tok_ref(x, L0_tok_W, L0_tok_b, L0_tok_pos)
    h = _layernorm(h + _L0_attn_ref(h, L0_attn_Wq, L0_attn_bq, L0_attn_Wk, L0_attn_bk, L0_attn_Wv, L0_attn_bv, L0_attn_Wo, L0_attn_bo), axis=-1)
    h = _layernorm(h + _L0_ffn_ref(h, L0_ffn_gate_w, L0_ffn_gate_b, L0_ffn_w1, L0_ffn_b1, L0_ffn_w2, L0_ffn_b2), axis=-1)
    return h

_drawn_inputs = setup_inputs


def setup_inputs(seed=0):
    import zlib

    import numpy as np

    out = dict(_drawn_inputs(seed))
    spreads = {'L0_ffn_gate_b': (0.0, 0.1), 'L0_ffn_b1': (0.0, 0.8), 'L0_ffn_b2': (0.0, 0.8)}
    factors = {'L0_attn_bq': 4.446, 'L0_attn_bk': 8.0}
    for name, (base, spread) in spreads.items():
        noise = np.random.default_rng([zlib.crc32(name.encode()), seed]).standard_normal(out[name].shape)
        drawn = base * np.exp(spread * noise) if base else spread * noise
        out[name] = jnp.asarray(drawn.astype(out[name].dtype))
    for name, factor in factors.items():
        out[name] = (out[name] * factor).astype(out[name].dtype)
    return out
```

```python
from contextlib import ExitStack

import numpy as np

import concourse.bass as bass
from concourse import mybir

F32 = mybir.dt.float32
F32R = mybir.dt.float32r
BF16 = mybir.dt.bfloat16
U32 = mybir.dt.uint32
ALU = mybir.AluOpType
ACT = mybir.ActivationFunctionType
AX = mybir.AxisListType

NB = 32
S = 1024
D = 64
PATCH = 49
P = 128
NT = S // P
T = NB * S
E = 8
FF = 256
CAP = -(-5 * T // (4 * E))
SLOTS = E * CAP
EPS = 1e-5
FAR = float(1 << 20)
FMAX = 3.4028235e38
ROW = D + 2
KTOK = D + 1 + PATCH
KA = D + 1
NG = E + 1
GV = D + NG + 2
GT = D + NG + 1
HALF = 512
CH = 1024
NCH = CAP // CH
NIN = 5
HB = FF // P


def build(nc, x, posT, tok_b, tok_wT, wqk, woT, wv, gw, bo_col, bv_col, bo_row, gb_row,
          w1, w2, b2, ident, centre, strict, sumcol, desc, slot0, tok0, out):
    slots = nc.dram_tensor("slots", (SLOTS, ROW), F32, kind="Internal").ap()
    with ExitStack() as ctx:
        def sb(name, shape, dt=F32):
            return ctx.enter_context(nc.sbuf_tensor(name, shape, dt))

        def ps(name, shape):
            return ctx.enter_context(nc.psum_tensor(name, shape, F32))

        def sem(name):
            return ctx.enter_context(nc.semaphore(name))

        c_id = sb("c_id", [P, P])
        c_centre = sb("c_centre", [D, D])
        c_strict = sb("c_strict", [P, P])
        c_sum = sb("c_sum", [P, 1])
        c_desc = sb("c_desc", [P, E])
        c_slot0 = sb("c_slot0", [P, E])
        c_tok = sb("c_tok", [P, NT])
        c_gb = sb("c_gb", [P, E])
        c_bo = sb("c_bo", [P, D])
        c_half = sb("c_half", [P, NT])
        c_neg = sb("c_neg", [E, E])
        id16 = sb("id16", [P, P], BF16)
        strict16 = sb("strict16", [P, P], BF16)
        ones16 = sb("ones16", [P, P], BF16)
        w_tok = sb("w_tok", [P, D])
        w_qk = sb("w_qk", [KA, 2 * D])
        w_oT = sb("w_oT", [D, D])
        w_oTp = sb("w_oTp", [D, D])
        w_v = sb("w_v", [D, D])
        w_g = sb("w_g", [D, E])
        w_bv = sb("w_bv", [D, 1])
        w_gm = sb("w_gm", [D, NG])
        w_bl = sb("w_bl", [D, KA])
        w_lj = sb("w_lj", [D, P])
        w_rj = sb("w_rj", [D, D + NG])
        w_va = sb("w_va", [KA, GV])
        w_j = sb("w_j", [P, GT])
        init = sb("init", [P, 20, ROW])

        xt = sb("xt", [P, 2, S])
        hT = sb("hT", [P, 2, S])
        hi = sb("hi", [P, S], F32R)
        lo = sb("lo", [P, S], F32R)
        mQ = [sb(f"mQ{i}", [P, S], F32R) for i in range(2)]
        sK = [sb(f"sK{i}", [P, S], F32R) for i in range(2)]
        mR = [sb(f"mR{i}", [P, S], F32R) for i in range(2)]
        sR = [sb(f"sR{i}", [P, S], F32R) for i in range(2)]
        mx = sb("mx", [P, 2, NT])
        pT = [sb(f"pT{i}", [P, S]) for i in range(4)]
        vv = sb("vv", [P, 2, NT, D])
        hh = sb("hh", [P, 2, NT, GV])
        uu = sb("uu", [P, S])
        rs = sb("rs", [P, NT])
        kz = sb("kz", [P, NT])
        mk = sb("mk", [P, NT])
        rm = sb("rm", [P, NT])
        tt = sb("tt", [P, NT, D + NG])
        t2 = sb("t2", [P, NT, D + NG])
        uc = sb("uc", [P, NT, D])
        sq = sb("sq", [P, NT, D])
        vs = sb("vs", [P, NT])
        ve = sb("ve", [P, 2, NT])
        vr = sb("vr", [P, NT])
        rstd = sb("rstd", [P, NT])
        rst2 = sb("rst2", [P, NT])
        lg = sb("lg", [P, NT, E])
        lb = sb("lb", [P, NT, E])
        lm = sb("lm", [P, NT])
        ld = sb("ld", [P, NT, E])
        ex = sb("ex", [P, NT, E])
        se = sb("se", [P, NT])
        pri = sb("pri", [P, NT, E])
        pm = sb("pm", [P, NT])
        oh = sb("oh", [P, NT, E], BF16)
        ohs = sb("ohs", [P, E], BF16)
        acc = sb("acc", [P, E], BF16)
        far = sb("far", [P, NT, E])
        pa = sb("pa", [P, NT, E])
        pb = sb("pb", [P, NT, E])
        pc = sb("pc", [P, NT, E])
        si = sb("si", [P, NT])
        idx = sb("idx", [P, 2, NT], U32)
        rows = sb("rows", [P, 2, NT, ROW])
        o0 = sb("o0", [P, 2, NT, D])

        b_w1 = sb("b_w1", [KA, 2, FF])
        b_w2 = sb("b_w2", [P, 2, HB, D])
        b_b2 = sb("b_b2", [P, 2, D])
        b_in = sb("b_in", [P, NIN, NT, ROW])
        b_xT = sb("b_xT", [P, CH])
        b_h = sb("b_h", [P, HB, CH])
        b_y = sb("b_y", [P, NT, D])
        b_m = sb("b_m", [P, 3, NT, D], mybir.dt.uint8)
        b_big = sb("b_big", [P, 3, D])
        b_p = sb("b_p", [P, NT, D])
        b_u = sb("b_u", [P, NT, D])
        b_mu = sb("b_mu", [P, NT])
        b_mm = sb("b_mm", [P, NT])
        b_c = sb("b_c", [P, NT, D])
        b_sq = sb("b_sq", [P, NT, D])
        b_vs = sb("b_vs", [P, NT])
        b_sd = sb("b_sd", [P, NT])
        b_rs = sb("b_rs", [P, NT])
        b_eps = sb("b_eps", [P, 1])
        b_o = sb("b_o", [P, 2, NT, D])
        b_ix = sb("b_ix", [P, 2, NT], U32)

        p_misc = ps("p_misc", [P, 2, HALF])
        p_sm = ps("p_sm", [P, 2, HALF])
        p_st = ps("p_st", [P, 2, HALF])
        p_u = ps("p_u", [P, 2, HALF])

        def flat(t):
            return t[:, :, :].rearrange("p a b -> p (a b)")

        def tiles(t, w):
            return t[:, :, 0:4 * w].rearrange("p a (t c) -> p a t c", c=w)

        def four(ap):
            return ap.rearrange("p (a t) c -> p a t c", a=2)

        def per_token(ap, n):
            return ap.unsqueeze(2).broadcast_to([P, NT, n])

        def per_column(ap, n):
            return ap.unsqueeze(1).broadcast_to([P, NT, n])

        slots_c = slots.rearrange("(c p j) w -> c p j w", p=P, j=NT)
        slots_i = slots.rearrange("(k p a) w -> k p (a w)", p=P, a=20)
        out_rows = out.rearrange("b s d -> (b s) d")
        p_y = [p_misc[:, i, :].rearrange("p (j d) -> p j d", d=D) for i in range(2)]
        turned = tiles(p_misc, GT)
        p_pos = p_misc[:, 1, 0:NT * E].rearrange("p (j e) -> p j e", e=E)
        p_hh = p_misc[:, 0, :].rearrange("p (j d) -> p j d", d=D)

        w_loaded = sem("w_loaded")
        x_loaded = [sem(f"x_loaded{i}") for i in range(2)]
        spread = [sem(f"spread{i}") for i in range(2)]
        init_stored = sem("init_stored")
        o0_stored = [sem(f"o0_stored{i}") for i in range(2)]
        scattered = [sem(f"scattered{i}") for i in range(2)]
        const_set = sem("const_set")
        pool_set = sem("pool_set")
        setup_v = sem("setup_v")
        setup_p = sem("setup_p")
        tok_done = sem("tok_done")
        h_ready = sem("h_ready")
        qk_done = sem("qk_done")
        hi_ready = sem("hi_ready")
        lo_ready = sem("lo_ready")
        v_done = sem("v_done")
        v_ready = sem("v_ready")
        hh_done = sem("hh_done")
        hh_ready = sem("hh_ready")
        sm_done = sem("sm_done")
        max_done = sem("max_done")
        mt_done = sem("mt_done")
        shift_ready = sem("shift_ready")
        st_done = sem("st_done")
        exp_done = sem("exp_done")
        pv_done = sem("pv_done")
        u_ready = sem("u_ready")
        turn_done = sem("turn_done")
        tail_v = sem("tail_v")
        t_ready = sem("t_ready")
        tail_g = sem("tail_g")
        uc_ready = sem("uc_ready")
        sq_ready = sem("sq_ready")
        vs_ready = sem("vs_ready")
        rstd_ready = sem("rstd_ready")
        gap_ready = sem("gap_ready")
        ex_ready = sem("ex_ready")
        oh_ready = sem("oh_ready")
        pos_done = sem("pos_done")
        pos_read = sem("pos_read")
        prob_ready = sem("prob_ready")
        o0_ready = sem("o0_ready")
        e_loaded = [sem(f"e_loaded{i}") for i in range(2)]
        c_loaded = [sem(f"c_loaded{i}") for i in range(NIN)]
        b_t_done = sem("b_t_done")
        b_xT_ready = sem("b_xT_ready")
        b_h_done = sem("b_h_done")
        b_relu = sem("b_relu")
        b_y_done = sem("b_y_done")
        b_y_read = sem("b_y_read")
        b_tail = sem("b_tail")
        b_c_ready = sem("b_c_ready")
        b_sq_ready = sem("b_sq_ready")
        b_vs_ready = sem("b_vs_ready")
        b_sd_ready = sem("b_sd_ready")
        b_o_ready = sem("b_o_ready")
        b_scattered = [sem(f"b_scattered{i}") for i in range(2)]

        set_link = sem("set_link")
        pool_step = sem("pool_step")
        POOL_SET = 2
        GS = 13
        NW = 21

        def of_parity(n, p, per):
            return (per // 2) * n + per - (per // 2) * p

        def run_windows(eng, step):
            def has(b):
                return lambda k: 0 <= b + k < NB
            for b in range(-2, 3):
                step(b, b % 2, has(b))
            with eng.Fori(0, (NB - 8) // 2) as i:
                step(2 * i + 3, 1, has(3))
                step(2 * i + 4, 0, has(3))
            for b in range(NB - 5, NB + 2):
                step(b, b % 2, has(b))

        def after(eng, s, value):
            if not isinstance(value, int) or value > 0:
                eng.wait_ge(s, value)

        def wait_apart(eng, s, value):
            if not isinstance(value, int):
                value = eng.lower_val(value)
                eng.wait_ge(w_loaded, 16 * NW)
            if not isinstance(value, int) or value > 0:
                eng.wait_ge(s, value)

        def run_pairs(eng, step):
            step(0, True, False)
            with eng.Fori(1, E // 2 - 1) as i:
                step(i, False, False)
            step(E // 2 - 1, False, True)

        def chunk_in(i, m):
            return 16 * (2 * NCH // NIN) * i + 16 * (m // NIN) + 16

        block = ctx.enter_context(nc.Block())

        @block.sync
        def _(sp):
            for dst, src in ((c_id[:, :], ident), (c_centre[:, :], centre), (c_strict[:, :], strict),
                             (c_sum[:, :], sumcol), (c_desc[:, :], desc), (c_slot0[:, :], slot0),
                             (c_tok[:, :], tok0), (c_gb[:, :], gb_row), (c_bo[:, :], bo_row),
                             (w_tok[0:D, :], ident[0:D, 0:D]), (w_tok[D:D + 1, :], tok_b),
                             (w_tok[KA:KTOK, :], tok_wT), (w_qk[:, :], wqk), (w_oT[:, :], woT),
                             (w_v[:, :], wv), (w_g[:, :], gw), (w_bv[:, :], bv_col),
                             (w_bl[:, 0:D], ident[0:D, 0:D]), (w_bl[:, D:KA], bo_col),
                             (xt[0:D, 0, :], posT), (xt[0:D, 1, :], posT)):
                sp.dma_start(dst, src).then_inc(w_loaded, 16)
            for p in range(2):
                sp.dma_start(xt[KA:KTOK, p, :], x[p, :, :]).then_inc(x_loaded[p], 16)

            def step(b, par, has):
                if has(4):
                    sp.wait_ge(tok_done, b + 3)
                    sp.dma_start(xt[KA:KTOK, par, :], x[b + 4, :, :]).then_inc(x_loaded[par], 16)
                if has(-1):
                    sp.wait_ge(o0_ready, b)
                    sp.dma_start(out[b - 1, :, :].rearrange("(p j) d -> p j d", j=NT),
                                 o0[:, 1 - par, :, :]).then_inc(o0_stored[1 - par], 16)
                if has(2):
                    sp.wait_ge(hi_ready, b + 3)
                    sp.wait_ge(lo_ready, b + 3)
                    if has(0):
                        sp.wait_ge(st_done, NT * b + NT)
                    for dst, src in ((mQ[par][0:D, :], hi[0:D, :]), (mQ[par][D:P, :], hi[0:D, :]),
                                     (sK[par][0:D, :], hi[D:P, :]), (sK[par][D:P, :], lo[D:P, :]),
                                     (mR[par][0:D, :], lo[0:D, :]), (sR[par][0:D, :], hi[D:P, :])):
                        sp.dma_start(dst.bitcast(F32), src.bitcast(F32)).then_inc(spread[par], 16)
            run_windows(sp, step)

            def load_expert(e, q):
                sp.dma_start(b_w1[:, q, :], w1[e, :, :]).then_inc(e_loaded[q], 16)
                sp.dma_start(b_w2[:, q, :, :], w2[e, :, :, :]).then_inc(e_loaded[q], 16)
                sp.dma_start(b_b2[:, q, :], b2[e, :, :]).then_inc(e_loaded[q], 16)

            def load_chunk(c, r):
                sp.dma_start(b_in[:, r, :, :], slots_c[c, :, :, :]).then_inc(c_loaded[r], 16)

            load_expert(0, 0)
            load_expert(1, 1)
            for p in range(2):
                sp.wait_ge(scattered[p], 16 * NT * NB // 2)
            for c in range(NIN):
                load_chunk(c, c)

            def pair(i, first, last):
                for m in range(2 * NCH):
                    if not (last and m + NIN >= 2 * NCH):
                        sp.wait_ge(b_o_ready, 2 * NCH * i + m + 1)
                        load_chunk(2 * NCH * i + m + NIN, m % NIN)
                    if not last and m % NCH == NCH - 1:
                        load_expert(2 * i + 2 + m // NCH, m // NCH)
            run_pairs(sp, pair)
            for p in range(2):
                sp.wait_ge(o0_stored[p], 16 * NB // 2)
                sp.wait_ge(b_scattered[p], 16 * NT * E * NCH // 2)

        @block.tensor
        def _(pe):
            pe.wait_ge(w_loaded, 16 * NW)
            pe.wait_ge(setup_v, 1)
            pe.matmul(p_misc[0:D, 0, 0:D], w_v[:, :], w_oTp[:, :], start=True, stop=True)
            pe.matmul(p_misc[0:D, 1, 0:E], c_centre[:, :], w_g[:, :], start=True, stop=True)
            pe.matmul(p_sm[0:D, 0, 0:1], w_oTp[:, :], w_bv[:, :], start=True, stop=True)\
                .then_inc(setup_p, 1)
            pe.wait_ge(setup_v, 2)
            pe.matmul(p_st[0:KA, 0, 0:NG], w_bl[:, :], w_gm[:, :], start=True, stop=True)
            pe.matmul(p_st[:, 1, 0:D + NG], w_lj[:, :], w_rj[:, :], start=True, stop=True)\
                .then_inc(setup_p, 1)
            pe.wait_ge(setup_v, 3)
            pe.wait_ge(const_set, 1)

            def token_product(n, p):
                pe.wait_ge(x_loaded[p], of_parity(n, p, 16))
                if isinstance(n, int) and n == 1:
                    pe.wait_ge(lo_ready, 1)
                after(pe, hh_ready, n - 1)
                after(pe, pos_read, n - 3)
                for a in range(2):
                    last = pe.matmul(p_misc[0:D, a, :], w_tok[0:KTOK, :],
                                     xt[0:KTOK, p, a * HALF:(a + 1) * HALF], start=True, stop=True)
                last.then_inc(tok_done, 1)

            def qk_product(n, p):
                pe.wait_ge(h_ready, n + 1)
                after(pe, t_ready, n - 2)
                for a in range(2):
                    last = pe.matmul(p_misc[:, a, :], w_qk[:, :],
                                     hT[0:KA, p, a * HALF:(a + 1) * HALF], start=True, stop=True)
                last.then_inc(qk_done, 1)

            def v_product(n, p, qk_next):
                if qk_next:
                    pe.wait_ge(lo_ready, n + 2)
                after(pe, t_ready, n - 1)
                for j in range(NT):
                    last = pe.matmul(p_misc[:, j // 4, (j % 4) * GV:(j % 4 + 1) * GV],
                                     hT[0:KA, p, j * P:(j + 1) * P], w_va[:, :], start=True, stop=True)
                last.then_inc(v_done, 1)

            def h_turn(n, p):
                wait_apart(pe, v_ready, n + 1)
                for j in range(NT):
                    last = pe.transpose(p_hh[:, j, :], hT[0:D, p, j * P:(j + 1) * P], c_id[0:D, 0:D])
                last.then_inc(hh_done, 1)

            def max_scores(n, p, j):
                if j == 0:
                    pe.wait_ge(spread[p], of_parity(n, p, 96))
                    after(pe, shift_ready, n)
                after(pe, max_done, NT * n + j)
                for a in range(2):
                    last = pe.matmul(p_sm[:, a, :], mQ[p][:, j * P:(j + 1) * P],
                                     sK[p][:, a * HALF:(a + 1) * HALF], start=True, stop=True)
                last.then_inc(sm_done, 1)

            def max_turn(n, p):
                wait_apart(pe, max_done, NT * n + NT)
                pe.transpose(p_sm[0:NT, 0, 0:P], mx[:, p, :], c_id[:, :]).then_inc(mt_done, 1)

            def scores(n, p, k):
                if k == 0:
                    pe.wait_ge(shift_ready, n + 1)
                after(pe, exp_done, NT * n + k)
                for a in range(2):
                    pe.matmul(p_st[:, a, :], sK[p][:, k * P:(k + 1) * P],
                              mQ[p][:, a * HALF:(a + 1) * HALF], start=True, stop=False)
                for a in range(2):
                    last = pe.matmul(p_st[:, a, :], sR[p][0:D + NT, k * P:(k + 1) * P],
                                     mR[p][0:D + NT, a * HALF:(a + 1) * HALF], start=False, stop=True)
                last.then_inc(st_done, 1)

            def weighted_sum(n, p, r):
                if r == 0:
                    pe.wait_ge(v_ready, n + 1)
                    after(pe, u_ready, n)
                pe.wait_ge(exp_done, NT * n + 2 * r + 2)
                for a in range(2):
                    for k in (2 * r, 2 * r + 1):
                        c = D * (k % 2)
                        last = pe.matmul(p_u[c:c + D, a, :], vv[:, p, k, :],
                                         pT[k % 4][:, a * HALF:(a + 1) * HALF],
                                         start=(r == 0), stop=(r == 3))
                last.then_inc(pv_done, 1)

            def turn_sums(n, next_tok):
                pe.wait_ge(u_ready, n + 1)
                if next_tok:
                    pe.wait_ge(h_ready, n + 4)
                else:
                    after(pe, hh_ready, min(n + 2, NB))
                    after(pe, pos_read, n)
                for j in range(NT):
                    last = pe.matmul(p_misc[:, j // 4, (j % 4) * GT:(j % 4 + 1) * GT],
                                     uu[:, j * P:(j + 1) * P], w_j[:, :], start=True, stop=True)
                last.then_inc(turn_done, 1)

            def positions(n, v_next):
                pe.wait_ge(oh_ready, n + 1)
                after(pe, tail_g, GS * n)
                if v_next:
                    pe.wait_ge(v_ready, n + 3)
                pe.wait_ge(t_ready, n + 1)
                pe.matmul(p_pos, ones16[:, :], per_column(acc[:, :], E), start=True, stop=False)
                for j in range(NT):
                    pe.matmul(p_pos[:, j:NT, :], id16[:, :],
                              oh[:, j, :].unsqueeze(1).broadcast_to([P, NT - j, E]),
                              start=False, stop=False, skip_group_check=j > 0)
                pe.matmul(p_pos, strict16[:, :], per_column(ohs[:, :], E), start=False, stop=True)\
                    .then_inc(pos_done, 1)

            def step(b, par, has):
                q = 1 - par
                if has(-1):
                    weighted_sum(b - 1, q, 3)
                if has(0):
                    max_turn(b, par)
                if has(2):
                    token_product(b + 2, par)
                if has(0):
                    scores(b, par, 0)
                if has(-1):
                    turn_sums(b - 1, has(2))
                if has(0):
                    scores(b, par, 1)
                if has(2):
                    qk_product(b + 2, par)
                for k in range(2, NT):
                    if has(1):
                        max_scores(b + 1, q, k - 2 + (k > 5))
                    if has(0):
                        scores(b, par, k)
                    if k % 2 == 0 and has(0):
                        weighted_sum(b, par, k // 2 - 1)
                    if k == 3 and has(1):
                        v_product(b + 1, q, has(2))
                    if k == 5 and has(1):
                        h_turn(b + 1, q)
                        max_scores(b + 1, q, 4)
                if has(1):
                    max_scores(b + 1, q, 7)
                if has(-1):
                    positions(b - 1, has(1))
            run_windows(pe, step)

            def rows_turn(i, m):
                c, r = 2 * NCH * i + m, m % NIN
                wait_apart(pe, c_loaded[r], chunk_in(i, m))
                wait_apart(pe, b_xT_ready, c)
                for j in range(NT):
                    last = pe.transpose(p_st[0:D, j // 4, (j % 4) * P:(j % 4 + 1) * P],
                                        b_in[:, r, j, 0:D], c_id[:, :])
                last.then_inc(b_t_done, 1)

            def hidden(c, q):
                pe.wait_ge(b_xT_ready, c + 1)
                for f in range(HB):
                    after(pe, b_relu, HB * c - HB + f + 1)
                    for a in range(2):
                        last = pe.matmul((p_sm, p_u)[f][:, a, :], b_w1[:, q, f * P:(f + 1) * P],
                                         b_xT[0:KA, a * HALF:(a + 1) * HALF], start=True, stop=True)
                    last.then_inc(b_h_done, 1)

            def pair(i, first, last):
                for m in range(2 * NCH):
                    c, q = 2 * NCH * i + m, m // NCH
                    if m % NCH == 0:
                        pe.wait_ge(e_loaded[q], 48 * (i + 1))
                    hidden(c, q)
                    if not (last and m == 2 * NCH - 1):
                        rows_turn(i, m + 1)
                    pe.wait_ge(b_relu, HB * c + HB)
                    after(pe, b_y_read, c - 1)
                    for j in range(NT):
                        for f in range(HB):
                            mm = pe.matmul(p_y[m % 2][:, j, :], b_h[:, f, j * P:(j + 1) * P],
                                           b_w2[:, q, f, :], start=(f == 0), stop=(f == HB - 1))
                    mm.then_inc(b_y_done, 1)
            rows_turn(0, 0)
            run_pairs(pe, pair)

        @block.scalar
        def _(act):
            act.wait_ge(setup_v, 3)

            def h_copy(n, p):
                act.wait_ge(tok_done, n + 1)
                after(act, hh_done, n - 1)
                act.activation(hT[0:D, p, :], flat(p_misc)[0:D, :], ACT.Copy).then_inc(h_ready, 1)

            def qk_high(n, p):
                act.wait_ge(qk_done, n + 1)
                if not isinstance(n, int) or n >= 1:
                    act.wait_ge(spread[1 - p], of_parity(n - 1, 1 - p, 96))
                act.activation(hi[:, :], flat(p_misc), ACT.Copy).then_inc(hi_ready, 1)

            def v_copy(n, p):
                act.wait_ge(v_done, n + 1)
                after(act, pv_done, 4 * n - 4)
                after(act, uc_ready, n - 1)
                pv = tiles(p_misc, GV)
                act.activation(four(vv[:, p, :, 0:D - 1]), pv[:, :, :, 0:D - 1], ACT.Copy)
                act.activation(four(hh[:, p, :, D:GV]), pv[:, :, :, D:GV], ACT.Copy)\
                    .then_inc(v_ready, 1)

            def exponent(n, k):
                act.wait_ge(st_done, NT * n + k + 1)
                after(act, pv_done, 4 * n + k // 2 - 1)
                act.activation(pT[k % 4][:, :], flat(p_st), ACT.Exp).then_inc(exp_done, 1)

            def u_copy(n):
                act.wait_ge(pv_done, 4 * n + 4)
                after(act, turn_done, n)
                act.activation(uu[:, :], flat(p_u), ACT.Copy).then_inc(u_ready, 1)

            def square(n):
                act.wait_ge(uc_ready, n + 1)
                after(act, vs_ready, n)
                act.activation(sq[:, :, :], uc[:, :, :], ACT.Square).then_inc(sq_ready, 1)

            def gate_exp(n):
                act.wait_ge(gap_ready, n + 1)
                after(act, prob_ready, n)
                act.activation(ex[:, :, :], ld[:, :, :], ACT.Exp).then_inc(ex_ready, 1)

            def step(b, par, has):
                q = 1 - par
                if has(-1):
                    u_copy(b - 1)
                if has(2):
                    h_copy(b + 2, par)
                for k in range(NT):
                    if has(0):
                        exponent(b, k)
                    if k == 1 and has(2):
                        qk_high(b + 2, par)
                    if k == 3:
                        if has(1):
                            v_copy(b + 1, q)
                        if has(-1):
                            square(b - 1)
                    if k == 5 and has(-1):
                        gate_exp(b - 1)
            run_windows(act, step)

            def xT_copy(c):
                act.wait_ge(b_t_done, c + 1)
                after(act, b_h_done, HB * c)
                act.activation(b_xT[0:D, :], flat(p_st)[0:D, :], ACT.Copy).then_inc(b_xT_ready, 1)

            def variance(c):
                act.wait_ge(b_c_ready, c + 1)
                act.activation(b_sq[:, :, :], b_c[:, :, :], ACT.Square).then_inc(b_sq_ready, 1)
                act.wait_ge(b_vs_ready, c + 1)
                act.activation(b_sd[:, :], b_vs[:, :], ACT.Sqrt, bias=b_eps[:, 0:1], scale=1.0 / D)\
                    .then_inc(b_sd_ready, 1)

            def pair(i, first, last):
                for m in range(2 * NCH):
                    c = 2 * NCH * i + m
                    after(act, b_y_done, c)
                    for f in range(HB):
                        act.wait_ge(b_h_done, HB * c + f + 1)
                        act.activation(b_h[:, f, :], flat((p_sm, p_u)[f]), ACT.Relu)\
                            .then_inc(b_relu, 1)
                    if not (last and m == 2 * NCH - 1):
                        xT_copy(c + 1)
                    if not (first and m == 0):
                        variance(c - 1)
            act.wait_ge(pool_set, POOL_SET)
            xT_copy(0)
            run_pairs(act, pair)
            variance(E * NCH - 1)

        @block.vector
        def _(dve):
            links = [0]

            def link(ins):
                links[0] += 1
                ins.then_inc(set_link, 1)
                dve.wait_ge(set_link, links[0])

            dve.memset(xt[D:KA, :, :], 1.0)
            dve.memset(hT[D:KA, :, :], 1.0)
            dve.memset(b_xT[D:KA, :], 1.0)
            dve.memset(vv[:, :, :, D - 1:D], 1.0)
            for p in range(2):
                dve.memset(sR[p][D:D + NT, :].bitcast(F32), 1.0)
            dve.memset(ones16[:, :], 1.0)
            dve.memset(c_half[:, :], -0.5)
            dve.memset(w_va[:, :], 0.0)
            dve.memset(w_gm[:, E:NG], 1.0 / D)
            dve.memset(b_eps[:, :], EPS)
            dve.memset(b_big[:, 0, :], 1e4)
            dve.memset(b_big[:, 1, :], -1e4)
            dve.memset(b_big[:, 2, :], 0.0)
            dve.memset(acc[:, :], 0.0).then_inc(const_set, 1)
            dve.wait_ge(const_set, 1)
            dve.wait_ge(w_loaded, 16 * NW)
            dve.tensor_scalar(w_oTp[:, :], w_oT[:, :], w_oT[:, D - 1:D], None, ALU.subtract)\
                .then_inc(setup_v, 1)
            dve.tensor_copy(id16[:, :], c_id[:, :])
            dve.tensor_copy(strict16[:, :], c_strict[:, :])
            dve.tensor_scalar(c_neg[:, :], c_id[0:E, 0:E], -1.0, None, ALU.mult)
            dve.tensor_copy(w_va[:, GV - 2:GV - 1], w_qk[:, 0:1])
            dve.tensor_copy(w_va[:, GV - 1:GV], w_qk[:, D:D + 1])
            dve.tensor_copy(w_j[:, GT - 1:GT], c_sum[:, :])
            dve.tensor_copy(w_lj[:, 0:D], c_id[0:D, 0:D])
            dve.tensor_copy(w_lj[:, D:P], c_id[0:D, 0:D])
            link(dve.tensor_copy(w_rj[:, 0:D], c_id[0:D, 0:D]))
            dve.tensor_scalar(w_qk[:, 0:D], w_qk[:, 0:D], D ** -0.5, None, ALU.mult)
            dve.wait_ge(setup_p, 1)
            dve.tensor_copy(w_va[0:D, 0:D], p_misc[0:D, 0, 0:D])
            dve.tensor_copy(w_gm[:, 0:E], p_misc[0:D, 1, 0:E])
            dve.tensor_copy(w_lj[:, D - 1:D], p_sm[0:D, 0, 0:1])
            link(dve.tensor_copy(w_lj[:, P - 1:P], p_sm[0:D, 0, 0:1]))
            dve.tensor_copy(w_rj[:, D:D + NG], w_gm[:, :]).then_inc(setup_v, 1)
            dve.wait_ge(setup_p, 2)
            dve.tensor_copy(w_va[:, D:D + NG], p_st[0:KA, 0, 0:NG])
            dve.tensor_copy(w_j[:, 0:D + NG], p_st[:, 1, 0:D + NG]).then_inc(setup_v, 1)

            def qk_low(n, p):
                dve.wait_ge(hi_ready, n + 1)
                if not isinstance(n, int) or n >= 1:
                    dve.wait_ge(spread[1 - p], of_parity(n - 1, 1 - p, 96))
                dve.tensor_tensor(lo[:, :], flat(p_misc), hi[:, :].bitcast(F32), ALU.subtract)\
                    .then_inc(lo_ready, 1)

            def residual(n, p):
                dve.wait_ge(hh_done, n + 1)
                after(dve, uc_ready, n - 1)
                dve.tensor_tensor(hh[:, p, :, 0:D], p_hh, per_column(c_bo[:, :], D), ALU.add)\
                    .then_inc(hh_ready, 1)

            def row_max(n, p, j):
                dve.wait_ge(sm_done, NT * n + j + 1)
                if j == 0:
                    after(dve, mt_done, n - 1)
                dve.tensor_reduce(mx[:, p, j:j + 1], flat(p_sm), AX.X, ALU.max).then_inc(max_done, 1)

            def shift(n, p):
                dve.wait_ge(mt_done, n + 1)
                after(dve, st_done, NT * n - NT)
                dve.tensor_tensor(
                    mR[p][D:D + NT, :].rearrange("p (b c) -> p b c", c=P),
                    p_sm[0:NT, 0, 0:P].unsqueeze(1).broadcast_to([NT, NT, P]),
                    c_neg[:, :].unsqueeze(2).broadcast_to([NT, NT, P]), ALU.mult).then_inc(shift_ready, 1)

            TS = 3

            def attend(n, p):
                def step(i, ins):
                    ins.then_inc(tail_v, 1)
                    dve.wait_ge(tail_v, TS * n + i)

                dve.wait_ge(turn_done, n + 1)
                dve.wait_ge(v_ready, n + 1)
                after(dve, uc_ready, n)
                dve.reciprocal(rs[:, :].rearrange("p (a t) -> p a t", a=2), turned[:, :, :, GT - 1])
                step(1, dve.tensor_scalar(kz[:, :], hh[:, p, :, GV - 1], 0.0, None, ALU.not_equal))
                step(2, dve.scalar_tensor_tensor(out=mk[:, :], in0=hh[:, p, :, GV - 2], scalar=0.0,
                                                 in1=kz[:, :], op0=ALU.not_equal, op1=ALU.mult))
                step(3, dve.tensor_tensor(rm[:, :], rs[:, :], mk[:, :], ALU.mult))
                dve.tensor_tensor(four(tt[:, :, :]), turned[:, :, :, 0:D + NG],
                                  four(per_token(rm[:, :], D + NG)), ALU.mult).then_inc(t_ready, 1)

            def sum_squares(n):
                dve.wait_ge(sq_ready, n + 1)
                after(dve, rstd_ready, n)
                dve.tensor_reduce(vs[:, :], sq[:, :, :], AX.X, ALU.add).then_inc(vs_ready, 1)

            def gate_step(n, i, ins):
                ins.then_inc(tail_g, 1)
                dve.wait_ge(tail_g, GS * n + i)

            def gate(n):
                dve.wait_ge(rstd_ready, n + 1)
                gate_step(n, 1, dve.tensor_tensor(lg[:, :, :], t2[:, :, D:D + E],
                                                  per_token(rstd[:, :], E), ALU.mult))
                gate_step(n, 2, dve.tensor_tensor(lb[:, :, :], lg[:, :, :],
                                                  per_column(c_gb[:, :], E), ALU.add))
                gate_step(n, 3, dve.tensor_reduce(lm[:, :], lb[:, :, :], AX.X, ALU.max))
                after(dve, ex_ready, n)
                dve.tensor_tensor(ld[:, :, :], lb[:, :, :], per_token(lm[:, :], E), ALU.subtract)\
                    .then_inc(gap_ready, 1)
                dve.wait_ge(gap_ready, n + 1)
                gate_step(n, 4, dve.scalar_tensor_tensor(
                    out=pri[:, :, :], in0=ld[:, :, :], scalar=0.0, in1=per_column(c_desc[:, :], E),
                    op0=ALU.is_equal, op1=ALU.mult))
                gate_step(n, 5, dve.tensor_reduce(pm[:, :], pri[:, :, :], AX.X, ALU.max))
                gate_step(n, 6, dve.tensor_tensor(oh[:, :, :], pri[:, :, :], per_token(pm[:, :], E),
                                                  ALU.is_equal))
                with nc.allow_low_precision("counts up to 8"):
                    dve.tensor_reduce(ohs[:, :], oh[:, :, :].rearrange("p j e -> p e j"), AX.X, ALU.add)\
                        .then_inc(oh_ready, 1)

            def probability(n, p):
                dve.wait_ge(ex_ready, n + 1)
                gate_step(n, 7, dve.tensor_reduce(se[:, :], ex[:, :, :], AX.X, ALU.add))
                after(dve, scattered[p], of_parity(n - 2, p, 16 * NT) if not isinstance(n, int) or n >= 2
                      else 0)
                dve.reciprocal(rows[:, p, :, D], se[:, :]).then_inc(prob_ready, 1)

            def slot_index(n, p):
                dve.wait_ge(pos_done, n + 1)
                gate_step(n, 8, dve.tensor_scalar(far[:, :, :], p_pos, float(CAP), FAR,
                                                  ALU.is_gt, ALU.mult))
                dve.tensor_tensor(pa[:, :, :], p_pos, far[:, :, :], ALU.add).then_inc(pos_read, 1)
                dve.wait_ge(pos_read, n + 1)
                gate_step(n, 9, dve.tensor_tensor(pb[:, :, :], pa[:, :, :],
                                                  per_column(c_slot0[:, :], E), ALU.add))
                gate_step(n, 10, dve.tensor_tensor(pc[:, :, :], pb[:, :, :], oh[:, :, :], ALU.mult))
                gate_step(n, 11, dve.tensor_reduce(si[:, :], pc[:, :, :], AX.X, ALU.add))
                gate_step(n, 12, dve.tensor_copy(idx[:, p, :], si[:, :]))
                with nc.allow_low_precision("counts up to 256"):
                    gate_step(n, 13, dve.tensor_tensor(acc[:, :], acc[:, :], ohs[:, :], ALU.add))

            def step(b, par, has):
                q = 1 - par
                if has(0):
                    shift(b, par)
                if has(-1):
                    attend(b - 1, q)
                if has(1):
                    row_max(b + 1, q, 0)
                if has(2):
                    qk_low(b + 2, par)
                if has(1):
                    for j in (1, 2, 3):
                        row_max(b + 1, q, j)
                if has(-1):
                    sum_squares(b - 1)
                if has(1):
                    residual(b + 1, q)
                    row_max(b + 1, q, 4)
                if has(-1):
                    gate(b - 1)
                if has(1):
                    row_max(b + 1, q, 5)
                if has(-1):
                    probability(b - 1, q)
                if has(1):
                    row_max(b + 1, q, 6)
                    row_max(b + 1, q, 7)
                if has(-1):
                    slot_index(b - 1, q)
            run_windows(dve, step)

            BS = 10

            def chunk(i, m):
                c, q, r = 2 * NCH * i + m, m // NCH, m % NIN
                rows_in = b_in[:, r, :, :]
                done = [0]

                def step(ins):
                    done[0] += 1
                    ins.then_inc(b_tail, 1)
                    wait_apart(dve, b_tail, BS * c + done[0])

                wait_apart(dve, b_y_done, c + 1)
                wait_apart(dve, e_loaded[q], 48 * i + 48)
                wait_apart(dve, c_loaded[r], chunk_in(i, m))
                dve.tensor_tensor(b_y[:, :, :], p_y[m % 2], per_column(b_b2[:, q, :], D), ALU.add)\
                    .then_inc(b_y_read, 1)
                dve.wait_ge(b_y_read, c + 1)
                dve.tensor_scalar(b_m[:, 0, :, :], b_y[:, :, :], FMAX, None, ALU.is_gt)
                dve.tensor_scalar(b_m[:, 1, :, :], b_y[:, :, :], -FMAX, None, ALU.is_lt)
                step(dve.tensor_tensor(b_m[:, 2, :, :], b_y[:, :, :], b_y[:, :, :], ALU.not_equal))
                for k in range(3):
                    step(dve.copy_predicated(b_y[:, :, :], b_m[:, k, :, :], per_column(b_big[:, k, :], D)))
                step(dve.tensor_tensor(b_p[:, :, :], b_y[:, :, :], per_token(rows_in[:, :, D], D), ALU.mult))
                step(dve.tensor_tensor(b_u[:, :, :], b_p[:, :, :], rows_in[:, :, 0:D], ALU.add))
                step(dve.tensor_reduce(b_mu[:, :], b_u[:, :, :], AX.X, ALU.add))
                step(dve.tensor_scalar(b_mm[:, :], b_mu[:, :], 1.0 / D, None, ALU.mult))
                after(dve, b_sq_ready, c)
                dve.tensor_tensor(b_c[:, :, :], b_u[:, :, :], per_token(b_mm[:, :], D), ALU.subtract)\
                    .then_inc(b_c_ready, 1)
                dve.wait_ge(b_sq_ready, c + 1)
                after(dve, b_sd_ready, c)
                dve.tensor_reduce(b_vs[:, :], b_sq[:, :, :], AX.X, ALU.add).then_inc(b_vs_ready, 1)
                if not (isinstance(i, int) and i == 0 and m < 2):
                    dve.wait_ge(b_scattered[m % 2], 16 * NT * (NCH * i + m // 2))
                step(dve.tensor_copy(b_ix[:, m % 2, :], rows_in[:, :, D + 1]))
                dve.wait_ge(b_sd_ready, c + 1)
                step(dve.reciprocal(b_rs[:, :], b_sd[:, :]))
                dve.tensor_tensor(b_o[:, m % 2, :, :], b_c[:, :, :], per_token(b_rs[:, :], D), ALU.mult)\
                    .then_inc(b_o_ready, 1)
                assert done[0] == BS, done[0]

            def pair(i, first, last):
                for m in range(2 * NCH):
                    chunk(i, m)
            run_pairs(dve, pair)

        @block.gpsimd
        def _(pool):
            pool.memset(init[:, :, :], 0.0).then_inc(pool_set, 1)
            pool.wait_ge(pool_set, 1)
            pool.memset(init[:, :, D + 1:ROW], FAR).then_inc(pool_set, 1)
            pool.wait_ge(pool_set, 2)
            for k in range(SLOTS // P // 20):
                pool.dma_start(slots_i[k, :, :], init[:, :, :].rearrange("p a w -> p (a w)"))\
                    .then_inc(init_stored, 16)
            pool.wait_ge(w_loaded, 16 * NW)
            pool.wait_ge(const_set, 1)
            pool.wait_ge(init_stored, 16 * (SLOTS // P // 20))

            PS = 7

            def tail(n, p):
                def step(i, ins):
                    ins.then_inc(pool_step, 1)
                    wait_apart(pool, pool_step, PS * n + i)

                wait_apart(pool, t_ready, n + 1)
                wait_apart(pool, hh_ready, n + 1)
                wait_apart(pool, oh_ready, n)
                step(1, pool.tensor_tensor(t2[:, :, :], tt[:, :, :], hh[:, p, :, 0:D + NG], ALU.add))
                after(pool, sq_ready, n)
                pool.tensor_tensor(uc[:, :, :], t2[:, :, 0:D], per_token(t2[:, :, D + E], D),
                                   ALU.subtract).then_inc(uc_ready, 1)
                wait_apart(pool, vs_ready, n + 1)
                step(2, pool.tensor_scalar(ve[:, 0, :], vs[:, :], 1.0 / D, EPS, ALU.mult, ALU.add))
                pool.tensor_tensor(rstd[:, :], ve[:, 0, :], c_half[:, :], ALU.pow).then_inc(rstd_ready, 1)
                step(3, pool.tensor_scalar(ve[:, 1, :], ve[:, 0, :], EPS, None, ALU.mult))
                step(4, pool.tensor_scalar(vr[:, :], vs[:, :], 1.0 / D, None, ALU.mult))
                step(5, pool.tensor_tensor(ve[:, 1, :], ve[:, 1, :], vr[:, :], ALU.add))
                step(6, pool.tensor_tensor(rst2[:, :], ve[:, 1, :], c_half[:, :], ALU.pow))
                if not isinstance(n, int) or n >= 2:
                    pool.wait_ge(scattered[p], of_parity(n - 2, p, 16 * NT))
                    pool.wait_ge(o0_stored[p], of_parity(n - 2, p, 16))
                pool.tensor_tensor(rows[:, p, :, 0:D], uc[:, :, :], per_token(rstd[:, :], D), ALU.mult)
                pool.tensor_copy(rows[:, p, :, D + 1], c_tok[:, :])
                pool.tensor_tensor(o0[:, p, :, :], uc[:, :, :], per_token(rst2[:, :], D), ALU.mult)\
                    .then_inc(o0_ready, 1)
                step(7, pool.tensor_scalar(c_tok[:, :], c_tok[:, :], float(S), None, ALU.add))

            def scatter(n, p):
                wait_apart(pool, prob_ready, n + 1)
                wait_apart(pool, tail_g, GS * n + GS)
                wait_apart(pool, o0_ready, n + 1)
                for j in range(NT):
                    pool.indirect_dma_start(slots, bass.IndirectOffsetOnAxis(ap=idx[:, p, j:j + 1], axis=0),
                                            rows[:, p, j, :], None, bounds_check=SLOTS - 1,
                                            oob_is_err=False).then_inc(scattered[p], 16)

            def step(b, par, has):
                if has(-2):
                    scatter(b - 2, par)
                if has(-1):
                    tail(b - 1, 1 - par)
            run_windows(pool, step)

            for p in range(2):
                pool.wait_ge(o0_stored[p], 16 * NB // 2)

            def pair(i, first, last):
                for m in range(2 * NCH):
                    wait_apart(pool, b_o_ready, 2 * NCH * i + m + 1)
                    for j in range(NT):
                        pool.indirect_dma_start(out_rows, bass.IndirectOffsetOnAxis(
                            ap=b_ix[:, m % 2, j:j + 1], axis=0), b_o[:, m % 2, j, :], None,
                            bounds_check=T - 1, oob_is_err=False).then_inc(b_scattered[m % 2], 16)
            run_pairs(pool, pair)


_INS = ["x", "posT", "tok_b", "tok_wT", "wqk", "woT", "wv", "gw", "bo_col", "bv_col", "bo_row", "gb_row",
        "w1", "w2", "b2", "ident", "centre", "strict", "sumcol", "desc", "slot0", "tok0"]


def kernel(x, L0_tok_W, L0_tok_b, L0_tok_pos, L0_attn_Wq, L0_attn_bq, L0_attn_Wk, L0_attn_bk, L0_attn_Wv,
           L0_attn_bv, L0_attn_Wo, L0_attn_bo, L0_ffn_gate_w, L0_ffn_gate_b, L0_ffn_w1, L0_ffn_b1,
           L0_ffn_w2, L0_ffn_b2):
    import concourse.bacc as bacc
    from concourse.bass_utils import run_bass_kernel_spmd

    n = 32
    f = np.float32

    def columns(a):
        return a.reshape(*a.shape[:-1], P, NT).swapaxes(-1, -2).reshape(a.shape)

    patches = np.asarray(x).reshape(NB, n, 7, n, 7).transpose(0, 2, 4, 1, 3).reshape(NB, PATCH, S)
    wq, wk = np.asarray(L0_attn_Wq), np.asarray(L0_attn_Wk)
    up = np.concatenate([np.asarray(L0_ffn_w1), np.asarray(L0_ffn_b1)[:, None, :]], axis=1)
    down = np.asarray(L0_ffn_w2).reshape(E, HB, P, D).transpose(0, 2, 1, 3)
    sumcol = np.zeros((P, 1), f)
    sumcol[[D - 1, P - 1]] = 1
    arrays = {
        "x": columns(patches),
        "posT": columns(np.asarray(L0_tok_pos)[0].T),
        "tok_b": np.asarray(L0_tok_b)[None, :],
        "tok_wT": np.asarray(L0_tok_W).T,
        "wqk": np.concatenate([np.concatenate([wq.T, wk.T], axis=1),
                               np.concatenate([np.asarray(L0_attn_bq), np.asarray(L0_attn_bk)])[None]]),
        "woT": np.asarray(L0_attn_Wo).T,
        "wv": np.asarray(L0_attn_Wv),
        "gw": np.asarray(L0_ffn_gate_w),
        "bo_col": np.asarray(L0_attn_bo)[:, None],
        "bv_col": np.asarray(L0_attn_bv)[:, None],
        "bo_row": np.broadcast_to(np.asarray(L0_attn_bo), (P, D)),
        "gb_row": np.broadcast_to(np.asarray(L0_ffn_gate_b), (P, E)),
        "w1": up,
        "w2": down,
        "b2": np.broadcast_to(np.asarray(L0_ffn_b2)[:, None, :], (E, P, D)),
        "ident": np.eye(P, dtype=f),
        "centre": np.eye(D, dtype=f) - f(1 / D),
        "strict": np.triu(np.ones((P, P), f), 1),
        "sumcol": sumcol,
        "desc": np.broadcast_to(np.arange(E, 0, -1, dtype=f), (P, E)),
        "slot0": np.broadcast_to(np.arange(E, dtype=f) * CAP - 1, (P, E)),
        "tok0": np.arange(S, dtype=f).reshape(P, NT),
    }
    nc = bacc.Bacc("TRN2", target_bir_lowering=False, num_devices=1)
    args, given = [], {}
    for name in _INS:
        a = np.ascontiguousarray(arrays[name])
        given[f"in_{name}"] = a
        args.append(nc.dram_tensor(f"in_{name}", a.shape, mybir.dt.from_np(a.dtype), kind="ExternalInput").ap())
    out = nc.dram_tensor("out_0", (NB, S, D), F32, kind="ExternalOutput").ap()
    build(nc, *args, out)
    r = run_bass_kernel_spmd(nc, [given], core_ids=[0])
    return r.results[0]["out_0"]
```

```python
from contextlib import ExitStack

import numpy as np

import concourse.bass as bass
from concourse import mybir

F32 = mybir.dt.float32
F32R = mybir.dt.float32r
BF16 = mybir.dt.bfloat16
U32 = mybir.dt.uint32
ALU = mybir.AluOpType
ACT = mybir.ActivationFunctionType
AX = mybir.AxisListType

NB = 32
S = 1024
D = 64
PATCH = 49
P = 128
NT = S // P
T = NB * S
E = 8
FF = 256
CAP = -(-5 * T // (4 * E))
SLOTS = E * CAP
EPS = 1e-5
FAR = float(1 << 20)
FMAX = 3.4028235e38
ROW = D + 2
KTOK = D + 1 + PATCH
KA = D + 1
CG = D + E
GH = CG + 2
GP = D - 1 + GH
GT = CG + 1
HALF = 512
CH = 1024
NCH = CAP // CH
NIN = 5
HB = FF // P


def build(nc, x, posT, tok_bc, tok_w, wqk, woT, wv, gw, bo_col, bv_col, gb_row,
          w1, w2, b2, ident, centre, strict, sumcol, desc, slot0, tok0, out):
    slots = nc.dram_tensor("slots", (SLOTS, ROW), F32, kind="Internal").ap()
    with ExitStack() as ctx:
        def sb(name, shape, dt=F32):
            return ctx.enter_context(nc.sbuf_tensor(name, shape, dt))

        def ps(name, shape):
            return ctx.enter_context(nc.psum_tensor(name, shape, F32))

        def sem(name):
            return ctx.enter_context(nc.semaphore(name))

        c_id = sb("c_id", [P, P])
        c_centre = sb("c_centre", [D, D])
        c_strict = sb("c_strict", [P, P])
        c_sum = sb("c_sum", [P, 1])
        c_desc = sb("c_desc", [P, E])
        c_slot0 = sb("c_slot0", [P, E])
        c_tok = sb("c_tok", [P, NT])
        c_gb = sb("c_gb", [P, E])
        c_half = sb("c_half", [P, NT])
        c_neg = sb("c_neg", [E, E])
        id16 = sb("id16", [P, P], BF16)
        strict16 = sb("strict16", [P, P], BF16)
        ones16 = sb("ones16", [P, P], BF16)
        w_e = sb("w_e", [KA, KTOK])
        w_qk = sb("w_qk", [KA, 2 * D])
        w_oT = sb("w_oT", [D, D])
        w_oTp = sb("w_oTp", [D, D])
        w_v = sb("w_v", [D, D])
        w_g = sb("w_g", [D, E])
        w_bv = sb("w_bv", [D, 1])
        w_cg = sb("w_cg", [D, CG])
        w_bl = sb("w_bl", [D, KA])
        w_lj = sb("w_lj", [D, P])
        w_all = sb("w_all", [KA, GP])
        w_qkx = sb("w_qkx", [KTOK, 2 * D])
        w_px = sb("w_px", [KTOK, GP])
        w_j = sb("w_j", [P, GT])
        init = sb("init", [P, 20, ROW])

        xt = sb("xt", [P, 2, S])
        hi = [sb(f"hi{i}", [P, S], F32R) for i in range(2)]
        lo = [sb(f"lo{i}", [P, S], F32R) for i in range(2)]
        mQ = [sb(f"mQ{i}", [P, S], F32R) for i in range(2)]
        sK = [sb(f"sK{i}", [P, S], F32R) for i in range(2)]
        mR = [sb(f"mR{i}", [P, S], F32R) for i in range(2)]
        sR = [sb(f"sR{i}", [P, S], F32R) for i in range(2)]
        mx = sb("mx", [P, 2, NT])
        pT = [sb(f"pT{i}", [P, S]) for i in range(4)]
        vv = sb("vv", [P, 2, NT, D])
        hh = sb("hh", [P, 2, NT, GH])
        uu = sb("uu", [P, S])
        rs = sb("rs", [P, NT])
        kz = sb("kz", [P, NT])
        mk = sb("mk", [P, NT])
        rm = sb("rm", [P, NT])
        tt = sb("tt", [P, NT, CG])
        uc = sb("uc", [P, NT, CG])
        sq = sb("sq", [P, NT, D])
        vs = sb("vs", [P, NT])
        ve = sb("ve", [P, 2, NT])
        vr = sb("vr", [P, NT])
        rstd = sb("rstd", [P, NT])
        rst2 = sb("rst2", [P, NT])
        lg = sb("lg", [P, NT, E])
        lb = sb("lb", [P, NT, E])
        lm = sb("lm", [P, NT])
        ld = sb("ld", [P, NT, E])
        ex = sb("ex", [P, NT, E])
        se = sb("se", [P, NT])
        pri = sb("pri", [P, NT, E])
        pm = sb("pm", [P, NT])
        oh = sb("oh", [P, NT, E], BF16)
        ohs = sb("ohs", [P, E], BF16)
        acc = sb("acc", [P, E], BF16)
        far = sb("far", [P, NT, E])
        pa = sb("pa", [P, NT, E])
        pb = sb("pb", [P, NT, E])
        pc = sb("pc", [P, NT, E])
        si = sb("si", [P, NT])
        idx = sb("idx", [P, 2, NT], U32)
        rows = sb("rows", [P, 2, NT, ROW])
        o0 = sb("o0", [P, 2, NT, D])

        b_w1 = sb("b_w1", [KA, 2, FF])
        b_w2 = sb("b_w2", [P, 2, HB, D])
        b_b2 = sb("b_b2", [P, 2, D])
        b_in = sb("b_in", [P, NIN, NT, ROW])
        b_xT = sb("b_xT", [P, CH])
        b_h = sb("b_h", [P, HB, CH])
        b_big = sb("b_big", [P, 3, D])
        b_eps = sb("b_eps", [P, 1])
        b_y = sb("b_y", [P, 2, NT, D])
        b_m = sb("b_m", [P, 2, 3, NT, D], mybir.dt.uint8)
        b_p = sb("b_p", [P, 2, NT, D])
        b_u = sb("b_u", [P, 2, NT, D])
        b_mu = sb("b_mu", [P, 2, NT])
        b_mm = sb("b_mm", [P, 2, NT])
        b_c = sb("b_c", [P, 2, NT, D])
        b_sq = sb("b_sq", [P, 2, NT, D])
        b_vs = sb("b_vs", [P, 2, NT])
        b_sd = sb("b_sd", [P, 2, NT])
        b_rs = sb("b_rs", [P, 2, NT])
        b_o = sb("b_o", [P, NIN, NT, D])
        b_ix = sb("b_ix", [P, NIN, NT], U32)

        p_misc = ps("p_misc", [P, 2, HALF])
        p_sm = ps("p_sm", [P, 2, HALF])
        p_st = ps("p_st", [P, 2, HALF])
        p_u = ps("p_u", [P, 2, HALF])

        def flat(t):
            return t[:, :, :].rearrange("p a b -> p (a b)")

        def tiles(t, w):
            return t[:, :, 0:4 * w].rearrange("p a (t c) -> p a t c", c=w)

        def four(ap):
            return ap.rearrange("p (a t) c -> p a t c", a=2)

        def per_token(ap, n):
            return ap.unsqueeze(2).broadcast_to([P, NT, n])

        def per_column(ap, n):
            return ap.unsqueeze(1).broadcast_to([P, NT, n])

        slots_c = slots.rearrange("(c p j) w -> c p j w", p=P, j=NT)
        slots_i = slots.rearrange("(k p a) w -> k p (a w)", p=P, a=20)
        out_rows = out.rearrange("b s d -> (b s) d")
        p_y = [p_misc[:, i, :].rearrange("p (j d) -> p j d", d=D) for i in range(2)]
        turned = tiles(p_misc, GT)
        p_pos = p_sm[:, 1, 0:NT * E].rearrange("p (j e) -> p j e", e=E)

        w_loaded = sem("w_loaded")
        x_loaded = [sem(f"x_loaded{i}") for i in range(2)]
        spread = [sem(f"spread{i}") for i in range(2)]
        init_stored = sem("init_stored")
        o0_stored = [sem(f"o0_stored{i}") for i in range(2)]
        scattered = [sem(f"scattered{i}") for i in range(2)]
        const_set = sem("const_set")
        pool_set = sem("pool_set")
        setup_v = sem("setup_v")
        setup_p = sem("setup_p")
        qk_done = sem("qk_done")
        hi_ready = sem("hi_ready")
        lo_ready = sem("lo_ready")
        v_done = sem("v_done")
        v_ready = sem("v_ready")
        sm_done = sem("sm_done")
        max_done = sem("max_done")
        mt_done = sem("mt_done")
        shift_ready = sem("shift_ready")
        st_done = sem("st_done")
        exp_done = sem("exp_done")
        pv_done = sem("pv_done")
        u_ready = sem("u_ready")
        turn_done = sem("turn_done")
        tail_v = sem("tail_v")
        t_ready = sem("t_ready")
        tail_g = sem("tail_g")
        uc_ready = sem("uc_ready")
        sq_ready = sem("sq_ready")
        vs_ready = sem("vs_ready")
        rstd_ready = sem("rstd_ready")
        gap_ready = sem("gap_ready")
        ex_ready = sem("ex_ready")
        oh_ready = sem("oh_ready")
        pos_done = sem("pos_done")
        pos_read = sem("pos_read")
        prob_ready = sem("prob_ready")
        o0_ready = sem("o0_ready")
        e_loaded = [sem(f"e_loaded{i}") for i in range(2)]
        c_loaded = [sem(f"c_loaded{i}") for i in range(NIN)]
        b_t_done = sem("b_t_done")
        b_xT_ready = sem("b_xT_ready")
        b_h_done = sem("b_h_done")
        b_relu = sem("b_relu")
        b_y_done = sem("b_y_done")
        b_y_read = sem("b_y_read")
        b_tail = sem("b_tail")
        b_c_ready = sem("b_c_ready")
        b_sq_ready = sem("b_sq_ready")
        b_vs_ready = sem("b_vs_ready")
        b_sd_ready = sem("b_sd_ready")
        b_o_ready = sem("b_o_ready")
        b_scattered = [sem(f"b_scattered{i}") for i in range(NIN)]

        set_link = sem("set_link")
        pool_step = sem("pool_step")
        POOL_SET = 2
        GS = 13
        NW = 20

        def of_parity(n, p, per):
            return (per // 2) * n + per - (per // 2) * p

        def run_windows(eng, step):
            def has(b):
                return lambda k: 0 <= b + k < NB
            for b in range(-2, 3):
                step(b, b % 2, has(b))
            with eng.Fori(0, (NB - 8) // 2) as i:
                step(2 * i + 3, 1, has(3))
                step(2 * i + 4, 0, has(3))
            for b in range(NB - 5, NB + 2):
                step(b, b % 2, has(b))

        def after(eng, s, value):
            if not isinstance(value, int) or value > 0:
                eng.wait_ge(s, value)

        def wait_apart(eng, s, value):
            if not isinstance(value, int):
                value = eng.lower_val(value)
                eng.wait_ge(w_loaded, 16 * NW)
            if not isinstance(value, int) or value > 0:
                eng.wait_ge(s, value)

        def run_pairs(eng, step):
            step(0, True, False)
            with eng.Fori(1, E // 2 - 1) as i:
                step(i, False, False)
            step(E // 2 - 1, False, True)

        def chunk_in(i, m):
            return 16 * (2 * NCH // NIN) * i + 16 * (m // NIN) + 16

        block = ctx.enter_context(nc.Block())

        @block.sync
        def _(sp):
            for dst, src in ((c_id[:, :], ident), (c_centre[:, :], centre), (c_strict[:, :], strict),
                             (c_sum[:, :], sumcol), (c_desc[:, :], desc), (c_slot0[:, :], slot0),
                             (c_tok[:, :], tok0), (c_gb[:, :], gb_row),
                             (w_e[0:D, 0:D], ident[0:D, 0:D]), (w_e[0:D, D:KA], tok_bc),
                             (w_e[0:D, KA:KTOK], tok_w), (w_qk[:, :], wqk), (w_oT[:, :], woT),
                             (w_v[:, :], wv), (w_g[:, :], gw), (w_bv[:, :], bv_col),
                             (w_bl[:, 0:D], ident[0:D, 0:D]), (w_bl[:, D:KA], bo_col),
                             (xt[0:D, 0, :], posT), (xt[0:D, 1, :], posT)):
                sp.dma_start(dst, src).then_inc(w_loaded, 16)
            for p in range(2):
                sp.dma_start(xt[KA:KTOK, p, :], x[p, :, :]).then_inc(x_loaded[p], 16)

            def step(b, par, has):
                if has(3) and has(1):
                    sp.wait_ge(v_done, 2 * b + 4)
                    sp.dma_start(xt[KA:KTOK, 1 - par, :], x[b + 3, :, :]).then_inc(x_loaded[1 - par], 16)
                if has(2):
                    sp.wait_ge(hi_ready, b + 3)
                    sp.wait_ge(lo_ready, b + 3)
                    if has(0):
                        sp.wait_ge(st_done, NT * b + NT)
                    for dst, src in ((mQ[par][0:D, :], hi[par][0:D, :]), (mQ[par][D:P, :], hi[par][0:D, :]),
                                     (sK[par][0:D, :], hi[par][D:P, :]), (sK[par][D:P, :], lo[par][D:P, :]),
                                     (mR[par][0:D, :], lo[par][0:D, :]), (sR[par][0:D, :], hi[par][D:P, :])):
                        sp.dma_start(dst.bitcast(F32), src.bitcast(F32)).then_inc(spread[par], 16)
                if has(-1):
                    sp.wait_ge(o0_ready, b)
                    sp.dma_start(out[b - 1, :, :].rearrange("(p j) d -> p j d", j=NT),
                                 o0[:, 1 - par, :, :]).then_inc(o0_stored[1 - par], 16)
            run_windows(sp, step)

            def load_expert(e, q):
                sp.dma_start(b_w1[:, q, :], w1[e, :, :]).then_inc(e_loaded[q], 16)
                sp.dma_start(b_w2[:, q, :, :], w2[e, :, :, :]).then_inc(e_loaded[q], 16)
                sp.dma_start(b_b2[:, q, :], b2[e, :, :]).then_inc(e_loaded[q], 16)

            def load_chunk(c, r):
                sp.dma_start(b_in[:, r, :, :], slots_c[c, :, :, :]).then_inc(c_loaded[r], 16)

            load_expert(0, 0)
            load_expert(1, 1)
            for p in range(2):
                sp.wait_ge(scattered[p], 16 * NT * NB // 2)
            for c in range(NIN):
                load_chunk(c, c)

            def pair(i, first, last):
                for m in range(2 * NCH):
                    if not (last and m + NIN >= 2 * NCH):
                        sp.wait_ge(b_o_ready, 2 * NCH * i + m + 1)
                        load_chunk(2 * NCH * i + m + NIN, m % NIN)
                    if not last and m % NCH == NCH - 1:
                        load_expert(2 * i + 2 + m // NCH, m // NCH)
            run_pairs(sp, pair)
            for p in range(2):
                sp.wait_ge(o0_stored[p], 16 * NB // 2)
            for r in range(NIN):
                sp.wait_ge(b_scattered[r], 16 * NT * E * NCH // NIN)

        @block.tensor
        def _(pe):
            pe.wait_ge(w_loaded, 16 * NW)
            pe.wait_ge(setup_v, 1)
            pe.matmul(p_misc[0:D, 0, 0:D], w_v[:, :], w_oTp[:, :], start=True, stop=True)
            pe.matmul(p_misc[0:D, 1, 0:E], c_centre[:, :], w_g[:, :], start=True, stop=True)
            pe.matmul(p_sm[0:D, 0, 0:1], w_oTp[:, :], w_bv[:, :], start=True, stop=True)\
                .then_inc(setup_p, 1)
            pe.wait_ge(setup_v, 2)
            pe.matmul(p_st[0:KA, 0, 0:CG], w_bl[:, :], w_cg[:, :], start=True, stop=True)
            pe.matmul(p_st[:, 1, 0:CG], w_lj[:, :], w_cg[:, :], start=True, stop=True)\
                .then_inc(setup_p, 1)
            pe.wait_ge(const_set, 1)
            pe.matmul(p_u[0:KTOK, 0, 0:2 * D], w_e[:, :], w_qk[:, :], start=True, stop=True)
            pe.wait_ge(setup_v, 3)
            pe.matmul(p_u[0:KTOK, 1, 0:GP], w_e[:, :], w_all[:, :], start=True, stop=True)\
                .then_inc(setup_p, 1)
            pe.wait_ge(setup_v, 4)

            def qk_product(n, p):
                pe.wait_ge(x_loaded[p], of_parity(n, p, 16))
                if isinstance(n, int) and n == 1:
                    pe.wait_ge(lo_ready, 1)
                after(pe, v_ready, 2 * n - 2)
                for a in range(2):
                    last = pe.matmul(p_misc[:, a, :], w_qkx[:, :],
                                     xt[0:KTOK, p, a * HALF:(a + 1) * HALF], start=True, stop=True)
                last.then_inc(qk_done, 1)

            def project(n, p, r, qk_next):
                if r == 0:
                    if qk_next:
                        pe.wait_ge(lo_ready, n + 2)
                    after(pe, t_ready, n - 1)
                else:
                    pe.wait_ge(v_ready, 2 * n + 1)
                for j in range(4):
                    t = 4 * r + j
                    last = pe.matmul(p_misc[:, j // 2, (j % 2) * GP:(j % 2 + 1) * GP],
                                     xt[0:KTOK, p, t * P:(t + 1) * P], w_px[:, :], start=True, stop=True)
                last.then_inc(v_done, 1)

            def max_scores(n, p, j):
                if j == 0:
                    pe.wait_ge(spread[p], of_parity(n, p, 96))
                    after(pe, shift_ready, n)
                    after(pe, pos_read, n - 2)
                after(pe, max_done, NT * n + j)
                for a in range(2):
                    last = pe.matmul(p_sm[:, a, :], mQ[p][:, j * P:(j + 1) * P],
                                     sK[p][:, a * HALF:(a + 1) * HALF], start=True, stop=True)
                last.then_inc(sm_done, 1)

            def max_turn(n, p):
                wait_apart(pe, max_done, NT * n + NT)
                pe.transpose(p_sm[0:NT, 0, 0:P], mx[:, p, :], c_id[:, :]).then_inc(mt_done, 1)

            def scores(n, p, k):
                if k == 0:
                    pe.wait_ge(shift_ready, n + 1)
                after(pe, exp_done, NT * n + k)
                for a in range(2):
                    pe.matmul(p_st[:, a, :], sK[p][:, k * P:(k + 1) * P],
                              mQ[p][:, a * HALF:(a + 1) * HALF], start=True, stop=False)
                for a in range(2):
                    last = pe.matmul(p_st[:, a, :], sR[p][0:D + NT, k * P:(k + 1) * P],
                                     mR[p][0:D + NT, a * HALF:(a + 1) * HALF], start=False, stop=True)
                last.then_inc(st_done, 1)

            def weighted_sum(n, p, r, halves=(0, 1)):
                if r == 0:
                    pe.wait_ge(v_ready, 2 * n + 2)
                    after(pe, u_ready, n)
                pe.wait_ge(exp_done, NT * n + 2 * r + 2)
                for a in halves:
                    for k in (2 * r, 2 * r + 1):
                        c = D * (k % 2)
                        last = pe.matmul(p_u[c:c + D, a, :], vv[:, p, k, :],
                                         pT[k % 4][:, a * HALF:(a + 1) * HALF],
                                         start=(r == 0), stop=(r == 3))
                if 1 in halves:
                    last.then_inc(pv_done, 1)

            def turn_sums(n, qk_next):
                pe.wait_ge(u_ready, n + 1)
                if qk_next:
                    pe.wait_ge(lo_ready, n + 4)
                else:
                    after(pe, v_ready, 2 * min(n + 2, NB))
                for j in range(NT):
                    last = pe.matmul(p_misc[:, j // 4, (j % 4) * GT:(j % 4 + 1) * GT],
                                     uu[:, j * P:(j + 1) * P], w_j[:, :], start=True, stop=True)
                last.then_inc(turn_done, 1)

            def positions(n):
                pe.wait_ge(oh_ready, n + 1)
                after(pe, tail_g, GS * n)
                pe.wait_ge(max_done, NT * min(n + 3, NB) if isinstance(n, int) else NT * n + 3 * NT)
                pe.matmul(p_pos, ones16[:, :], per_column(acc[:, :], E), start=True, stop=False)
                for j in range(NT):
                    pe.matmul(p_pos[:, j:NT, :], id16[:, :],
                              oh[:, j, :].unsqueeze(1).broadcast_to([P, NT - j, E]),
                              start=False, stop=False, skip_group_check=j > 0)
                pe.matmul(p_pos, strict16[:, :], per_column(ohs[:, :], E), start=False, stop=True)\
                    .then_inc(pos_done, 1)

            def step(b, par, has):
                q = 1 - par
                if has(0):
                    max_turn(b, par)
                if has(-2):
                    positions(b - 2)
                if has(2):
                    qk_product(b + 2, par)
                for k in range(NT):
                    if has(0):
                        scores(b, par, k)
                    if has(-1):
                        if k == 0:
                            weighted_sum(b - 1, q, 3)
                        if k == 1:
                            turn_sums(b - 1, has(2))
                    if k == 2 and has(0):
                        weighted_sum(b, par, 0, (0,))
                    if has(1):
                        max_scores(b + 1, q, k)
                        if k in (3, 6):
                            project(b + 1, q, k // 6, has(2))
                    if has(0):
                        if k == 2:
                            weighted_sum(b, par, 0, (1,))
                        if k in (4, 5):
                            weighted_sum(b, par, 1, (k - 4,))
                        if k == 7:
                            weighted_sum(b, par, 2)
            run_windows(pe, step)

            def rows_turn(i, m):
                c, r = 2 * NCH * i + m, m % NIN
                wait_apart(pe, c_loaded[r], chunk_in(i, m))
                wait_apart(pe, b_xT_ready, c)
                for j in range(NT):
                    last = pe.transpose(p_st[0:D, j // 4, (j % 4) * P:(j % 4 + 1) * P],
                                        b_in[:, r, j, 0:D], c_id[:, :])
                last.then_inc(b_t_done, 1)

            def hidden(c, q):
                pe.wait_ge(b_xT_ready, c + 1)
                for f in range(HB):
                    after(pe, b_relu, HB * c - HB + f + 1)
                    for a in range(2):
                        last = pe.matmul((p_sm, p_u)[f][:, a, :], b_w1[:, q, f * P:(f + 1) * P],
                                         b_xT[0:KA, a * HALF:(a + 1) * HALF], start=True, stop=True)
                    last.then_inc(b_h_done, 1)

            def pair(i, first, last):
                for m in range(2 * NCH):
                    c, q = 2 * NCH * i + m, m // NCH
                    if m % NCH == 0:
                        pe.wait_ge(e_loaded[q], 48 * (i + 1))
                    hidden(c, q)
                    if not (last and m == 2 * NCH - 1):
                        rows_turn(i, m + 1)
                    pe.wait_ge(b_relu, HB * c + HB)
                    after(pe, b_y_read, c - 1)
                    for j in range(NT):
                        for f in range(HB):
                            mm = pe.matmul(p_y[m % 2][:, j, :], b_h[:, f, j * P:(j + 1) * P],
                                           b_w2[:, q, f, :], start=(f == 0), stop=(f == HB - 1))
                    mm.then_inc(b_y_done, 1)
            rows_turn(0, 0)
            run_pairs(pe, pair)

        @block.scalar
        def _(act):
            act.wait_ge(setup_v, 4)

            def qk_high(n, p):
                act.wait_ge(qk_done, n + 1)
                if not isinstance(n, int) or n >= 2:
                    act.wait_ge(spread[p], of_parity(n - 2, p, 96))
                act.activation(hi[p][:, :], flat(p_misc), ACT.Copy).then_inc(hi_ready, 1)

            def v_copy(n, p, r):
                act.wait_ge(v_done, 2 * n + r + 1)
                if r == 0:
                    after(act, pv_done, 4 * n - 4)
                    after(act, uc_ready, n - 1)
                pv = p_misc[:, :, 0:2 * GP].rearrange("p a (t c) -> p a t c", c=GP)
                t = slice(4 * r, 4 * r + 4)
                act.activation(vv[:, p, t, 0:D - 1].rearrange("p (a t) c -> p a t c", a=2),
                               pv[:, :, :, 0:D - 1], ACT.Copy)
                act.activation(hh[:, p, t, :].rearrange("p (a t) c -> p a t c", a=2),
                               pv[:, :, :, D - 1:GP], ACT.Copy).then_inc(v_ready, 1)

            def exponent(n, k):
                act.wait_ge(st_done, NT * n + k + 1)
                after(act, pv_done, 4 * n + k // 2 - 1)
                act.activation(pT[k % 4][:, :], flat(p_st), ACT.Exp).then_inc(exp_done, 1)

            def u_copy(n):
                act.wait_ge(pv_done, 4 * n + 4)
                after(act, turn_done, n)
                act.activation(uu[:, :], flat(p_u), ACT.Copy).then_inc(u_ready, 1)

            def square(n):
                act.wait_ge(uc_ready, n + 1)
                after(act, vs_ready, n)
                act.activation(sq[:, :, :], uc[:, :, 0:D], ACT.Square).then_inc(sq_ready, 1)

            def gate_exp(n):
                act.wait_ge(gap_ready, n + 1)
                after(act, prob_ready, n)
                act.activation(ex[:, :, :], ld[:, :, :], ACT.Exp).then_inc(ex_ready, 1)

            def step(b, par, has):
                q = 1 - par
                if has(2):
                    qk_high(b + 2, par)
                for k in range(NT):
                    if k == 1 and has(-1):
                        u_copy(b - 1)
                    if k == 3 and has(-1):
                        square(b - 1)
                    if has(0):
                        exponent(b, k)
                    if k == 6 and has(-1):
                        gate_exp(b - 1)
                    if k in (3, 6) and has(1):
                        v_copy(b + 1, q, k // 6)
            run_windows(act, step)

            def xT_copy(c):
                act.wait_ge(b_t_done, c + 1)
                after(act, b_h_done, HB * c)
                act.activation(b_xT[0:D, :], flat(p_st)[0:D, :], ACT.Copy).then_inc(b_xT_ready, 1)

            def variance(c):
                for h in range(2):
                    act.wait_ge(b_c_ready, c + h + 1)
                    act.activation(b_sq[:, h, :, :], b_c[:, h, :, :], ACT.Square).then_inc(b_sq_ready, 1)
                for h in range(2):
                    act.wait_ge(b_vs_ready, c + h + 1)
                    act.activation(b_sd[:, h, :], b_vs[:, h, :], ACT.Sqrt, bias=b_eps[:, 0:1], scale=1.0 / D)\
                        .then_inc(b_sd_ready, 1)

            def pair(i, first, last):
                for m in range(2 * NCH):
                    c = 2 * NCH * i + m
                    after(act, b_y_done, c)
                    for f in range(HB):
                        act.wait_ge(b_h_done, HB * c + f + 1)
                        act.activation(b_h[:, f, :], flat((p_sm, p_u)[f]), ACT.Relu)\
                            .then_inc(b_relu, 1)
                    if not (last and m == 2 * NCH - 1):
                        xT_copy(c + 1)
                    if m % 2 == 1 and not (first and m == 1):
                        variance(c - 3)
            act.wait_ge(pool_set, POOL_SET)
            xT_copy(0)
            run_pairs(act, pair)
            variance(E * NCH - 2)

        @block.vector
        def _(dve):
            links = [1]

            def link(ins):
                links[0] += 1
                ins.then_inc(set_link, 1)
                dve.wait_ge(set_link, links[0])

            dve.memset(xt[D:KA, :, :], 1.0)
            dve.memset(b_xT[D:KA, :], 1.0)
            dve.memset(vv[:, :, :, D - 1:D], 1.0)
            for p in range(2):
                dve.memset(sR[p][D:D + NT, :].bitcast(F32), 1.0)
            dve.memset(ones16[:, :], 1.0)
            dve.memset(c_half[:, :], -0.5)
            dve.memset(w_all[:, :], 0.0)
            dve.memset(w_e[D:KA, :], 0.0).then_inc(set_link, 1)
            dve.wait_ge(set_link, 1)
            dve.memset(w_e[D:KA, D:KA], 1.0)
            dve.memset(b_eps[:, :], EPS)
            dve.memset(b_big[:, 0, :], 1e4)
            dve.memset(b_big[:, 1, :], -1e4)
            dve.memset(b_big[:, 2, :], 0.0)
            dve.memset(acc[:, :], 0.0).then_inc(const_set, 1)
            dve.wait_ge(const_set, 1)
            dve.wait_ge(w_loaded, 16 * NW)
            dve.tensor_scalar(w_oTp[:, :], w_oT[:, :], w_oT[:, D - 1:D], None, ALU.subtract)\
                .then_inc(setup_v, 1)
            dve.tensor_copy(id16[:, :], c_id[:, :])
            dve.tensor_copy(strict16[:, :], c_strict[:, :])
            dve.tensor_scalar(c_neg[:, :], c_id[0:E, 0:E], -1.0, None, ALU.mult)
            dve.tensor_copy(w_all[:, GP - 2:GP - 1], w_qk[:, 0:1])
            dve.tensor_copy(w_all[:, GP - 1:GP], w_qk[:, D:D + 1])
            dve.tensor_copy(w_j[:, GT - 1:GT], c_sum[:, :])
            dve.tensor_copy(w_cg[:, 0:D], c_centre[:, :])
            dve.tensor_copy(w_lj[:, 0:D], c_id[0:D, 0:D])
            link(dve.tensor_copy(w_lj[:, D:P], c_id[0:D, 0:D]))
            dve.wait_ge(setup_p, 1)
            dve.tensor_copy(w_all[0:D, 0:D - 1], p_misc[0:D, 0, 0:D - 1])
            dve.tensor_copy(w_cg[:, D:CG], p_misc[0:D, 1, 0:E])
            dve.tensor_copy(w_lj[:, D - 1:D], p_sm[0:D, 0, 0:1])
            dve.tensor_copy(w_lj[:, P - 1:P], p_sm[0:D, 0, 0:1]).then_inc(setup_v, 1)
            dve.wait_ge(setup_p, 2)
            dve.tensor_copy(w_all[:, D - 1:D - 1 + CG], p_st[0:KA, 0, 0:CG])
            dve.tensor_copy(w_j[:, 0:CG], p_st[:, 1, 0:CG]).then_inc(setup_v, 1)
            dve.wait_ge(setup_p, 3)
            dve.tensor_scalar(w_qkx[:, 0:D], p_u[0:KTOK, 0, 0:D], D ** -0.5, None, ALU.mult)
            dve.tensor_copy(w_qkx[:, D:2 * D], p_u[0:KTOK, 0, D:2 * D])
            dve.tensor_copy(w_px[:, :], p_u[0:KTOK, 1, 0:GP]).then_inc(setup_v, 1)

            def qk_low(n, p):
                dve.wait_ge(hi_ready, n + 1)
                if not isinstance(n, int) or n >= 2:
                    dve.wait_ge(spread[p], of_parity(n - 2, p, 96))
                dve.tensor_tensor(lo[p][:, :], flat(p_misc), hi[p][:, :].bitcast(F32), ALU.subtract)\
                    .then_inc(lo_ready, 1)

            def row_max(n, p, j):
                dve.wait_ge(sm_done, NT * n + j + 1)
                if j == 0:
                    after(dve, mt_done, n - 1)
                dve.tensor_reduce(mx[:, p, j:j + 1], flat(p_sm), AX.X, ALU.max).then_inc(max_done, 1)

            def shift(n, p):
                dve.wait_ge(mt_done, n + 1)
                after(dve, st_done, NT * n - NT)
                dve.tensor_tensor(
                    mR[p][D:D + NT, :].rearrange("p (b c) -> p b c", c=P),
                    p_sm[0:NT, 0, 0:P].unsqueeze(1).broadcast_to([NT, NT, P]),
                    c_neg[:, :].unsqueeze(2).broadcast_to([NT, NT, P]), ALU.mult).then_inc(shift_ready, 1)

            TS = 3

            def attend(n, p):
                def step(i, ins):
                    ins.then_inc(tail_v, 1)
                    dve.wait_ge(tail_v, TS * n + i)

                dve.wait_ge(turn_done, n + 1)
                dve.wait_ge(v_ready, 2 * n + 2)
                after(dve, uc_ready, n)
                dve.reciprocal(rs[:, :].rearrange("p (a t) -> p a t", a=2), turned[:, :, :, GT - 1])
                step(1, dve.tensor_scalar(kz[:, :], hh[:, p, :, GH - 1], 0.0, None, ALU.not_equal))
                step(2, dve.scalar_tensor_tensor(out=mk[:, :], in0=hh[:, p, :, GH - 2], scalar=0.0,
                                                 in1=kz[:, :], op0=ALU.not_equal, op1=ALU.mult))
                step(3, dve.tensor_tensor(rm[:, :], rs[:, :], mk[:, :], ALU.mult))
                dve.tensor_tensor(four(tt[:, :, :]), turned[:, :, :, 0:CG],
                                  four(per_token(rm[:, :], CG)), ALU.mult).then_inc(t_ready, 1)

            def sum_squares(n):
                dve.wait_ge(sq_ready, n + 1)
                after(dve, rstd_ready, n)
                dve.tensor_reduce(vs[:, :], sq[:, :, :], AX.X, ALU.add).then_inc(vs_ready, 1)

            def gate_step(n, i, ins):
                ins.then_inc(tail_g, 1)
                dve.wait_ge(tail_g, GS * n + i)

            def gate_logits(n):
                dve.wait_ge(rstd_ready, n + 1)
                gate_step(n, 1, dve.tensor_tensor(lg[:, :, :], uc[:, :, D:CG],
                                                  per_token(rstd[:, :], E), ALU.mult))
                gate_step(n, 2, dve.tensor_tensor(lb[:, :, :], lg[:, :, :],
                                                  per_column(c_gb[:, :], E), ALU.add))
                gate_step(n, 3, dve.tensor_reduce(lm[:, :], lb[:, :, :], AX.X, ALU.max))

            def gate_gaps(n):
                after(dve, ex_ready, n)
                dve.tensor_tensor(ld[:, :, :], lb[:, :, :], per_token(lm[:, :], E), ALU.subtract)\
                    .then_inc(gap_ready, 1)
                dve.wait_ge(gap_ready, n + 1)
                gate_step(n, 4, dve.scalar_tensor_tensor(
                    out=pri[:, :, :], in0=ld[:, :, :], scalar=0.0, in1=per_column(c_desc[:, :], E),
                    op0=ALU.is_equal, op1=ALU.mult))
                gate_step(n, 5, dve.tensor_reduce(pm[:, :], pri[:, :, :], AX.X, ALU.max))

            def gate_choice(n):
                gate_step(n, 6, dve.tensor_tensor(oh[:, :, :], pri[:, :, :], per_token(pm[:, :], E),
                                                  ALU.is_equal))
                with nc.allow_low_precision("counts up to 8"):
                    dve.tensor_reduce(ohs[:, :], oh[:, :, :].rearrange("p j e -> p e j"), AX.X, ALU.add)\
                        .then_inc(oh_ready, 1)

            def probability(n, p):
                dve.wait_ge(ex_ready, n + 1)
                gate_step(n, 7, dve.tensor_reduce(se[:, :], ex[:, :, :], AX.X, ALU.add))
                after(dve, scattered[p], of_parity(n - 2, p, 16 * NT) if not isinstance(n, int) or n >= 2
                      else 0)
                dve.reciprocal(rows[:, p, :, D], se[:, :]).then_inc(prob_ready, 1)

            def slot_index(n, p):
                dve.wait_ge(pos_done, n + 1)
                gate_step(n, 8, dve.tensor_scalar(far[:, :, :], p_pos, float(CAP), FAR,
                                                  ALU.is_gt, ALU.mult))
                dve.tensor_tensor(pa[:, :, :], p_pos, far[:, :, :], ALU.add).then_inc(pos_read, 1)
                dve.wait_ge(pos_read, n + 1)
                gate_step(n, 9, dve.tensor_tensor(pb[:, :, :], pa[:, :, :],
                                                  per_column(c_slot0[:, :], E), ALU.add))
                gate_step(n, 10, dve.tensor_tensor(pc[:, :, :], pb[:, :, :], oh[:, :, :], ALU.mult))
                gate_step(n, 11, dve.tensor_reduce(si[:, :], pc[:, :, :], AX.X, ALU.add))
                gate_step(n, 12, dve.tensor_copy(idx[:, p, :], si[:, :]))
                with nc.allow_low_precision("counts up to 256"):
                    gate_step(n, 13, dve.tensor_tensor(acc[:, :], acc[:, :], ohs[:, :], ALU.add))

            def step(b, par, has):
                q = 1 - par
                if has(0):
                    shift(b, par)
                if has(-2):
                    probability(b - 2, par)
                    slot_index(b - 2, par)
                if has(2):
                    qk_low(b + 2, par)
                for j in range(NT):
                    if has(1):
                        row_max(b + 1, q, j)
                    if has(-1):
                        if j == 1:
                            attend(b - 1, q)
                        if j == 2:
                            sum_squares(b - 1)
                        if j == 4:
                            gate_logits(b - 1)
                        if j == 5:
                            gate_gaps(b - 1)
                        if j == 6:
                            gate_choice(b - 1)
            run_windows(dve, step)

            BS = 20

            def two_chunks(i, m0):
                c0 = 2 * NCH * i + m0
                base = BS * (NCH * i + m0 // 2)
                done = [0]

                def count(ins):
                    done[0] += 1
                    ins.then_inc(b_tail, 1)

                def before(since=1):
                    wait_apart(dve, b_tail, base + done[0] - since)

                for h in range(2):
                    m = m0 + h
                    wait_apart(dve, b_y_done, c0 + h + 1)
                    wait_apart(dve, e_loaded[m // NCH], 48 * i + 48)
                    wait_apart(dve, c_loaded[m % NIN], chunk_in(i, m))
                    dve.tensor_tensor(b_y[:, h, :, :], p_y[m % 2], per_column(b_b2[:, m // NCH, :], D),
                                      ALU.add).then_inc(b_y_read, 1)
                for h in range(2):
                    dve.wait_ge(b_y_read, c0 + h + 1)
                    y = b_y[:, h, :, :]
                    dve.tensor_scalar(b_m[:, h, 0, :, :], y, FMAX, None, ALU.is_gt)
                    dve.tensor_scalar(b_m[:, h, 1, :, :], y, -FMAX, None, ALU.is_lt)
                    count(dve.tensor_tensor(b_m[:, h, 2, :, :], y, y, ALU.not_equal))
                for k in range(3):
                    for h in range(2):
                        before()
                        count(dve.copy_predicated(b_y[:, h, :, :], b_m[:, h, k, :, :],
                                                  per_column(b_big[:, k, :], D)))
                for h in range(2):
                    before()
                    count(dve.tensor_tensor(b_p[:, h, :, :], b_y[:, h, :, :],
                                            per_token(b_in[:, (m0 + h) % NIN, :, D], D), ALU.mult))
                for h in range(2):
                    before()
                    count(dve.tensor_tensor(b_u[:, h, :, :], b_p[:, h, :, :],
                                            b_in[:, (m0 + h) % NIN, :, 0:D], ALU.add))
                for h in range(2):
                    before()
                    count(dve.tensor_reduce(b_mu[:, h, :], b_u[:, h, :, :], AX.X, ALU.add))
                for h in range(2):
                    before()
                    count(dve.tensor_scalar(b_mm[:, h, :], b_mu[:, h, :], 1.0 / D, None, ALU.mult))
                for h in range(2):
                    before(1 - h)
                    after(dve, b_sq_ready, c0 + h - 1)
                    dve.tensor_tensor(b_c[:, h, :, :], b_u[:, h, :, :], per_token(b_mm[:, h, :], D),
                                      ALU.subtract).then_inc(b_c_ready, 1)
                for h in range(2):
                    r = (m0 + h) % NIN
                    if not (isinstance(i, int) and i == 0 and m0 + h < NIN):
                        wait_apart(dve, b_scattered[r], 16 * NT * ((2 * NCH // NIN) * i + (m0 + h) // NIN))
                    count(dve.tensor_copy(b_ix[:, r, :], b_in[:, r, :, D + 1]))
                for h in range(2):
                    dve.wait_ge(b_sq_ready, c0 + h + 1)
                    after(dve, b_sd_ready, c0 + h - 1)
                    dve.tensor_reduce(b_vs[:, h, :], b_sq[:, h, :, :], AX.X, ALU.add).then_inc(b_vs_ready, 1)
                for h in range(2):
                    dve.wait_ge(b_sd_ready, c0 + h + 1)
                    count(dve.reciprocal(b_rs[:, h, :], b_sd[:, h, :]))
                for h in range(2):
                    before(1 - h)
                    dve.tensor_tensor(b_o[:, (m0 + h) % NIN, :, :], b_c[:, h, :, :],
                                      per_token(b_rs[:, h, :], D), ALU.mult).then_inc(b_o_ready, 1)
                assert done[0] == BS, done[0]

            def pair(i, first, last):
                for m in range(0, 2 * NCH, 2):
                    two_chunks(i, m)
            run_pairs(dve, pair)

        @block.gpsimd
        def _(pool):
            pool.memset(init[:, :, :], 0.0).then_inc(pool_set, 1)
            pool.wait_ge(pool_set, 1)
            pool.memset(init[:, :, D + 1:ROW], FAR).then_inc(pool_set, 1)
            pool.wait_ge(pool_set, 2)
            for k in range(SLOTS // P // 20):
                pool.dma_start(slots_i[k, :, :], init[:, :, :].rearrange("p a w -> p (a w)"))\
                    .then_inc(init_stored, 16)
            pool.wait_ge(w_loaded, 16 * NW)
            pool.wait_ge(const_set, 1)
            pool.wait_ge(init_stored, 16 * (SLOTS // P // 20))

            PS = 6

            def residual(n, p):
                wait_apart(pool, t_ready, n + 1)
                wait_apart(pool, v_ready, 2 * n + 2)
                wait_apart(pool, oh_ready, n)
                wait_apart(pool, sq_ready, n)
                pool.tensor_tensor(uc[:, :, :], tt[:, :, :], hh[:, p, :, 0:CG], ALU.add)\
                    .then_inc(uc_ready, 1)

            def tail(n, p):
                def step(i, ins):
                    ins.then_inc(pool_step, 1)
                    wait_apart(pool, pool_step, PS * n + i)

                wait_apart(pool, vs_ready, n + 1)
                step(1, pool.tensor_scalar(ve[:, 0, :], vs[:, :], 1.0 / D, EPS, ALU.mult, ALU.add))
                pool.tensor_tensor(rstd[:, :], ve[:, 0, :], c_half[:, :], ALU.pow).then_inc(rstd_ready, 1)
                step(2, pool.tensor_scalar(ve[:, 1, :], ve[:, 0, :], EPS, None, ALU.mult))
                step(3, pool.tensor_scalar(vr[:, :], vs[:, :], 1.0 / D, None, ALU.mult))
                step(4, pool.tensor_tensor(ve[:, 1, :], ve[:, 1, :], vr[:, :], ALU.add))
                step(5, pool.tensor_tensor(rst2[:, :], ve[:, 1, :], c_half[:, :], ALU.pow))
                if not isinstance(n, int) or n >= 2:
                    pool.wait_ge(scattered[p], of_parity(n - 2, p, 16 * NT))
                    pool.wait_ge(o0_stored[p], of_parity(n - 2, p, 16))
                pool.tensor_tensor(rows[:, p, :, 0:D], uc[:, :, 0:D], per_token(rstd[:, :], D), ALU.mult)
                pool.tensor_copy(rows[:, p, :, D + 1], c_tok[:, :])
                pool.tensor_tensor(o0[:, p, :, :], uc[:, :, 0:D], per_token(rst2[:, :], D), ALU.mult)\
                    .then_inc(o0_ready, 1)
                step(6, pool.tensor_scalar(c_tok[:, :], c_tok[:, :], float(S), None, ALU.add))

            def scatter(n, p, tiles):
                if 0 in tiles:
                    wait_apart(pool, prob_ready, n + 1)
                    wait_apart(pool, tail_g, GS * n + GS)
                    wait_apart(pool, o0_ready, n + 1)
                for j in tiles:
                    pool.indirect_dma_start(slots, bass.IndirectOffsetOnAxis(ap=idx[:, p, j:j + 1], axis=0),
                                            rows[:, p, j, :], None, bounds_check=SLOTS - 1,
                                            oob_is_err=False).then_inc(scattered[p], 16)

            def step(b, par, has):
                if has(-2):
                    scatter(b - 2, par, range(6))
                if has(-1):
                    residual(b - 1, 1 - par)
                if has(-2):
                    scatter(b - 2, par, range(6, NT))
                if has(-1):
                    tail(b - 1, 1 - par)
            run_windows(pool, step)

            for p in range(2):
                pool.wait_ge(o0_stored[p], 16 * NB // 2)

            def pair(i, first, last):
                for m in range(2 * NCH):
                    wait_apart(pool, b_o_ready, 2 * NCH * i + m + 1)
                    for j in range(NT):
                        pool.indirect_dma_start(out_rows, bass.IndirectOffsetOnAxis(
                            ap=b_ix[:, m % NIN, j:j + 1], axis=0), b_o[:, m % NIN, j, :], None,
                            bounds_check=T - 1, oob_is_err=False).then_inc(b_scattered[m % NIN], 16)
            run_pairs(pool, pair)


_INS = ["x", "posT", "tok_bc", "tok_w", "wqk", "woT", "wv", "gw", "bo_col", "bv_col", "gb_row",
        "w1", "w2", "b2", "ident", "centre", "strict", "sumcol", "desc", "slot0", "tok0"]


def kernel(x, L0_tok_W, L0_tok_b, L0_tok_pos, L0_attn_Wq, L0_attn_bq, L0_attn_Wk, L0_attn_bk, L0_attn_Wv,
           L0_attn_bv, L0_attn_Wo, L0_attn_bo, L0_ffn_gate_w, L0_ffn_gate_b, L0_ffn_w1, L0_ffn_b1,
           L0_ffn_w2, L0_ffn_b2):
    import concourse.bacc as bacc
    from concourse.bass_utils import run_bass_kernel_spmd

    n = 32
    f = np.float32

    def columns(a):
        return a.reshape(*a.shape[:-1], P, NT).swapaxes(-1, -2).reshape(a.shape)

    patches = np.asarray(x).reshape(NB, n, 7, n, 7).transpose(0, 2, 4, 1, 3).reshape(NB, PATCH, S)
    wq, wk = np.asarray(L0_attn_Wq), np.asarray(L0_attn_Wk)
    up = np.concatenate([np.asarray(L0_ffn_w1), np.asarray(L0_ffn_b1)[:, None, :]], axis=1)
    down = np.asarray(L0_ffn_w2).reshape(E, HB, P, D).transpose(0, 2, 1, 3)
    sumcol = np.zeros((P, 1), f)
    sumcol[[D - 1, P - 1]] = 1
    arrays = {
        "x": columns(patches),
        "posT": columns(np.asarray(L0_tok_pos)[0].T),
        "tok_bc": np.asarray(L0_tok_b)[:, None],
        "tok_w": np.asarray(L0_tok_W),
        "wqk": np.concatenate([np.concatenate([wq.T, wk.T], axis=1),
                               np.concatenate([np.asarray(L0_attn_bq), np.asarray(L0_attn_bk)])[None]]),
        "woT": np.asarray(L0_attn_Wo).T,
        "wv": np.asarray(L0_attn_Wv),
        "gw": np.asarray(L0_ffn_gate_w),
        "bo_col": np.asarray(L0_attn_bo)[:, None],
        "bv_col": np.asarray(L0_attn_bv)[:, None],
        "gb_row": np.broadcast_to(np.asarray(L0_ffn_gate_b), (P, E)),
        "w1": up,
        "w2": down,
        "b2": np.broadcast_to(np.asarray(L0_ffn_b2)[:, None, :], (E, P, D)),
        "ident": np.eye(P, dtype=f),
        "centre": np.eye(D, dtype=f) - f(1 / D),
        "strict": np.triu(np.ones((P, P), f), 1),
        "sumcol": sumcol,
        "desc": np.broadcast_to(np.arange(E, 0, -1, dtype=f), (P, E)),
        "slot0": np.broadcast_to(np.arange(E, dtype=f) * CAP - 1, (P, E)),
        "tok0": np.arange(S, dtype=f).reshape(P, NT),
    }
    nc = bacc.Bacc("TRN2", target_bir_lowering=False, num_devices=1)
    args, given = [], {}
    for name in _INS:
        a = np.ascontiguousarray(arrays[name])
        given[f"in_{name}"] = a
        args.append(nc.dram_tensor(f"in_{name}", a.shape, mybir.dt.from_np(a.dtype), kind="ExternalInput").ap())
    out = nc.dram_tensor("out_0", (NB, S, D), F32, kind="ExternalOutput").ap()
    build(nc, *args, out)
    r = run_bass_kernel_spmd(nc, [given], core_ids=[0])
    return r.results[0]["out_0"]
```

```python
from contextlib import ExitStack

import numpy as np

import concourse.bass as bass
from concourse import mybir

F32 = mybir.dt.float32
F32R = mybir.dt.float32r
BF16 = mybir.dt.bfloat16
U32 = mybir.dt.uint32
ALU = mybir.AluOpType
ACT = mybir.ActivationFunctionType
AX = mybir.AxisListType

NB = 32
S = 1024
D = 64
PATCH = 49
P = 128
NT = S // P
T = NB * S
E = 8
FF = 256
CAP = -(-5 * T // (4 * E))
SLOTS = E * CAP
EPS = 1e-5
FAR = float(1 << 20)
FMAX = 3.4028235e38
ROW = D + 2
KTOK = D + 1 + PATCH
KA = D + 1
CG = D + E
GH = CG + 2
GP = D - 1 + GH
GT = CG + 1
HALF = 512
CH = 1024
NCH = CAP // CH
NIN = 5
HB = FF // P
WIDE = (P, P, 1, E, E, NT, E)
DEEP = (KTOK, D, D, D, E, 1, KA)
AI = 20
NINIT = SLOTS // P // AI


def build(nc, x, posT, wqk, wide, deep, w1, w2, b2, out):
    slots = nc.dram_tensor("slots", (SLOTS, ROW), F32, kind="Internal").ap()
    with ExitStack() as ctx:
        def sb(name, shape, dt=F32):
            return ctx.enter_context(nc.sbuf_tensor(name, shape, dt))

        def ps(name, shape):
            return ctx.enter_context(nc.psum_tensor(name, shape, F32))

        def sem(name):
            return ctx.enter_context(nc.semaphore(name))

        def views(tile, widths):
            at, parts = 0, []
            for w in widths:
                parts.append(tile[:, at:at + w])
                at += w
            return parts

        c_wide = sb("c_wide", [P, sum(WIDE)])
        c_deep = sb("c_deep", [D, sum(DEEP)])
        c_id, c_strict, c_sum, c_desc, c_slot0, c_tok, c_gb = views(c_wide, WIDE)
        w_t, c_centre, w_v, w_oT, w_g, w_bv, w_bl = views(c_deep, DEEP)
        c_half = sb("c_half", [P, NT])
        c_neg = sb("c_neg", [E, E])
        id16 = sb("id16", [P, P], BF16)
        strict16 = sb("strict16", [P, P], BF16)
        ones16 = sb("ones16", [P, P], BF16)
        w_e = sb("w_e", [KA, KTOK])
        w_qk = sb("w_qk", [KA, 2 * D])
        w_oTp = sb("w_oTp", [D, D])
        w_cg = sb("w_cg", [D, CG])
        w_lj = sb("w_lj", [D, P])
        w_all = sb("w_all", [KA, GP])
        w_qkx = sb("w_qkx", [KTOK, 2 * D])
        w_qkh = sb("w_qkh", [KTOK, 2 * D], F32R)
        w_qkl = sb("w_qkl", [KTOK, 2 * D], F32R)
        w_px = sb("w_px", [KTOK, GP])
        w_j = sb("w_j", [P, GT])
        init = sb("init", [P, AI, ROW])

        xt = sb("xt", [P, 2, S])
        xr = sb("xr", [P, S])
        xh = sb("xh", [P, S], F32R)
        xl = sb("xl", [P, S], F32R)
        hi = [sb(f"hi{i}", [P, S], F32R) for i in range(2)]
        lo = [sb(f"lo{i}", [P, S], F32R) for i in range(2)]
        mQ = [sb(f"mQ{i}", [P, S], F32R) for i in range(2)]
        sK = [sb(f"sK{i}", [P, S], F32R) for i in range(2)]
        mR = [sb(f"mR{i}", [P, S], F32R) for i in range(2)]
        sR = [sb(f"sR{i}", [P, S], F32R) for i in range(2)]
        mx = sb("mx", [P, 2, NT])
        pT = [sb(f"pT{i}", [P, S]) for i in range(4)]
        vv = sb("vv", [P, 2, NT, D])
        hh = sb("hh", [P, 2, NT, GH])
        uu = sb("uu", [P, S])
        rs = sb("rs", [P, NT])
        kz = sb("kz", [P, NT])
        mk = sb("mk", [P, NT])
        rm = sb("rm", [P, NT])
        tt = sb("tt", [P, NT, CG])
        uc = sb("uc", [P, NT, CG])
        sq = sb("sq", [P, NT, D])
        vs = sb("vs", [P, NT])
        ve = sb("ve", [P, 2, NT])
        vr = sb("vr", [P, NT])
        rstd = sb("rstd", [P, NT])
        rst2 = sb("rst2", [P, NT])
        lg = sb("lg", [P, NT, E])
        lb = sb("lb", [P, NT, E])
        lm = sb("lm", [P, NT])
        ld = sb("ld", [P, NT, E])
        ex = sb("ex", [P, NT, E])
        se = sb("se", [P, NT])
        pri = sb("pri", [P, NT, E])
        pm = sb("pm", [P, NT])
        oh = sb("oh", [P, NT, E], BF16)
        ohs = sb("ohs", [P, E], BF16)
        acc = sb("acc", [P, E], BF16)
        far = sb("far", [P, NT, E])
        pa = sb("pa", [P, NT, E])
        pb = sb("pb", [P, NT, E])
        pc = sb("pc", [P, NT, E])
        si = sb("si", [P, NT])
        idx = sb("idx", [P, 2, NT], U32)
        rows = sb("rows", [P, 2, NT, ROW])
        o0 = sb("o0", [P, 2, NT, D])

        b_w1 = sb("b_w1", [KA, 2, FF])
        b_w2 = sb("b_w2", [P, 2, HB, D])
        b_b2 = sb("b_b2", [P, 2, D])
        b_in = sb("b_in", [P, NIN, NT, ROW])
        b_xT = sb("b_xT", [P, CH])
        b_h = sb("b_h", [P, HB, CH])
        b_big = sb("b_big", [P, 3, D])
        b_eps = sb("b_eps", [P, 1])
        b_y = sb("b_y", [P, 2, NT, D])
        b_m = sb("b_m", [P, 3, NT, D], mybir.dt.uint8)
        b_p = sb("b_p", [P, NT, D])
        b_u = sb("b_u", [P, NT, D])
        b_mu = sb("b_mu", [P, NT])
        b_mm = sb("b_mm", [P, NT])
        b_c = sb("b_c", [P, NT, D])
        b_sq = sb("b_sq", [P, NT, D])
        b_vs = sb("b_vs", [P, NT])
        b_sd = sb("b_sd", [P, NT])
        b_rs = sb("b_rs", [P, NT])
        b_o = sb("b_o", [P, NIN, NT, D])
        b_ix = sb("b_ix", [P, NIN, NT], U32)

        p_misc = ps("p_misc", [P, 2, HALF])
        p_sm = ps("p_sm", [P, 2, HALF])
        p_st = ps("p_st", [P, 2, HALF])
        p_u = ps("p_u", [P, 2, HALF])

        def flat(t):
            return t[:, :, :].rearrange("p a b -> p (a b)")

        def tiles(t, w):
            return t[:, :, 0:4 * w].rearrange("p a (t c) -> p a t c", c=w)

        def four(ap):
            return ap.rearrange("p (a t) c -> p a t c", a=2)

        def per_token(ap, n):
            return ap.unsqueeze(2).broadcast_to([P, NT, n])

        def per_column(ap, n):
            return ap.unsqueeze(1).broadcast_to([P, NT, n])

        slots_c = slots.rearrange("(c p j) w -> c p j w", p=P, j=NT)
        slots_i = slots.rearrange("(k p a) w -> k p (a w)", p=P, a=AI)
        out_rows = out.rearrange("b s d -> (b s) d")
        p_y = [p_misc[:, i, :].rearrange("p (j d) -> p j d", d=D) for i in range(2)]
        turned = tiles(p_misc, GT)
        p_pos = p_sm[:, 1, 0:NT * E].rearrange("p (j e) -> p j e", e=E)

        w_loaded = sem("w_loaded")
        x_loaded = [sem(f"x_loaded{i}") for i in range(2)]
        spread = [sem(f"spread{i}") for i in range(2)]
        init_stored = sem("init_stored")
        o0_stored = [sem(f"o0_stored{i}") for i in range(2)]
        scattered = [sem(f"scattered{i}") for i in range(2)]
        const_set = sem("const_set")
        pool_set = sem("pool_set")
        setup_v = sem("setup_v")
        setup_p = sem("setup_p")
        raw_loaded = sem("raw_loaded")
        xh_ready = sem("xh_ready")
        xl_ready = sem("xl_ready")
        qk_done = sem("qk_done")
        hi_ready = sem("hi_ready")
        lo_ready = sem("lo_ready")
        v_done = sem("v_done")
        v_ready = sem("v_ready")
        sm_done = sem("sm_done")
        max_done = sem("max_done")
        mt_done = sem("mt_done")
        shift_ready = sem("shift_ready")
        st_done = sem("st_done")
        exp_done = sem("exp_done")
        pv_done = sem("pv_done")
        u_ready = sem("u_ready")
        turn_done = sem("turn_done")
        tail_v = sem("tail_v")
        t_ready = sem("t_ready")
        tail_g = sem("tail_g")
        uc_ready = sem("uc_ready")
        sq_ready = sem("sq_ready")
        vs_ready = sem("vs_ready")
        rstd_ready = sem("rstd_ready")
        gap_ready = sem("gap_ready")
        ex_ready = sem("ex_ready")
        oh_ready = sem("oh_ready")
        pos_done = sem("pos_done")
        pos_read = sem("pos_read")
        prob_ready = sem("prob_ready")
        o0_ready = sem("o0_ready")
        e_loaded = [sem(f"e_loaded{i}") for i in range(2)]
        c_loaded = [sem(f"c_loaded{i}") for i in range(NIN)]
        b_t_done = sem("b_t_done")
        b_xT_ready = sem("b_xT_ready")
        b_h_done = sem("b_h_done")
        b_relu = sem("b_relu")
        b_y_done = sem("b_y_done")
        b_y_read = sem("b_y_read")
        b_tail = sem("b_tail")
        b_c_ready = sem("b_c_ready")
        b_sq_ready = sem("b_sq_ready")
        b_vs_ready = sem("b_vs_ready")
        b_sd_ready = sem("b_sd_ready")
        b_o_ready = sem("b_o_ready")
        b_scattered = [sem(f"b_scattered{i}") for i in range(NIN)]

        set_link = sem("set_link")
        pool_step = sem("pool_step")
        POOL_SET = 2
        GS = 13
        NW = 5

        def of_parity(n, p, per):
            return (per // 2) * n + per - (per // 2) * p

        def run_windows(eng, step):
            def has(b):
                return lambda k: 0 <= b + k < NB
            for b in range(-2, 3):
                step(b, b % 2, has(b))
            with eng.Fori(0, (NB - 8) // 2) as i:
                step(2 * i + 3, 1, has(3))
                step(2 * i + 4, 0, has(3))
            for b in range(NB - 5, NB + 2):
                step(b, b % 2, has(b))

        def max_place(n, j):
            return p_st if isinstance(n, int) and n == 0 and j % 2 else p_sm

        def after(eng, s, value):
            if not isinstance(value, int) or value > 0:
                eng.wait_ge(s, value)

        def wait_apart(eng, s, value):
            if not isinstance(value, int):
                value = eng.lower_val(value)
                eng.wait_ge(w_loaded, 16 * NW)
            if not isinstance(value, int) or value > 0:
                eng.wait_ge(s, value)

        def run_pairs(eng, step):
            step(0, True, False)
            with eng.Fori(1, E // 2 - 1) as i:
                step(i, False, False)
            step(E // 2 - 1, False, True)

        def chunk_in(i, m):
            return 16 * (2 * NCH // NIN) * i + 16 * (m // NIN) + 16

        block = ctx.enter_context(nc.Block())

        @block.sync
        def _(sp):
            for dst, src in ((c_deep[:, :], deep), (w_qk[:, :], wqk), (c_wide[:, :], wide),
                             (xt[0:D, 0, :], posT), (xt[0:D, 1, :], posT)):
                sp.dma_start(dst, src).then_inc(w_loaded, 16)
            for p in range(2):
                sp.dma_start(xt[KA:KTOK, p, :], x[p, :, :]).then_inc(x_loaded[p], 16)

            sp.dma_start(xr[KA:KTOK, :], x[1, :, :]).then_inc(raw_loaded, 16)

            def store_default(n, p):
                sp.wait_ge(o0_ready, n + 1)
                sp.dma_start(out[n, :, :].rearrange("(p j) d -> p j d", j=NT), o0[:, p, :, :])\
                    .then_inc(o0_stored[p], 16)

            def load_patches(n, p):
                sp.wait_ge(v_done, 2 * n - 2)
                sp.dma_start(xt[KA:KTOK, p, :], x[n, :, :]).then_inc(x_loaded[p], 16)

            def step(b, par, has):
                if has(4):
                    sp.wait_ge(xl_ready, b + 4)
                    sp.dma_start(xr[KA:KTOK, :], x[b + 4, :, :]).then_inc(raw_loaded, 16)
                if has(3) and has(0):
                    load_patches(b + 3, 1 - par)
                if has(2):
                    sp.wait_ge(hi_ready, b + 3)
                    sp.wait_ge(lo_ready, b + 3)
                    if has(0):
                        sp.wait_ge(st_done, NT * b + NT)
                    for dst, src in ((mQ[par][0:D, :], hi[par][0:D, :]), (mQ[par][D:P, :], hi[par][0:D, :]),
                                     (sK[par][0:D, :], hi[par][D:P, :]), (sK[par][D:P, :], lo[par][D:P, :]),
                                     (mR[par][0:D, :], lo[par][0:D, :]), (sR[par][0:D, :], hi[par][D:P, :])):
                        sp.dma_start(dst.bitcast(F32), src.bitcast(F32)).then_inc(spread[par], 16)
                if has(3) and has(1) and not has(0):
                    load_patches(b + 3, 1 - par)
                if has(-1) and has(0):
                    store_default(b - 1, 1 - par)
            run_windows(sp, step)

            def load_expert(e, q):
                sp.dma_start(b_w1[:, q, :], w1[e, :, :]).then_inc(e_loaded[q], 16)
                sp.dma_start(b_w2[:, q, :, :], w2[e, :, :, :]).then_inc(e_loaded[q], 16)
                sp.dma_start(b_b2[:, q, :], b2[e, :, :]).then_inc(e_loaded[q], 16)

            def load_chunk(c, r):
                sp.dma_start(b_in[:, r, :, :], slots_c[c, :, :, :]).then_inc(c_loaded[r], 16)

            load_expert(0, 0)
            load_expert(1, 1)
            for p in range(2):
                sp.wait_ge(scattered[p], 16 * NT * NB // 2)
            for c in range(NIN):
                load_chunk(c, c)
            store_default(NB - 1, (NB - 1) % 2)

            def pair(i, first, last):
                for m in range(2 * NCH):
                    if not (last and m + NIN >= 2 * NCH):
                        sp.wait_ge(b_o_ready, 2 * NCH * i + m + 1)
                        load_chunk(2 * NCH * i + m + NIN, m % NIN)
                    if not last and m % NCH == NCH - 1:
                        load_expert(2 * i + 2 + m // NCH, m // NCH)
            run_pairs(sp, pair)
            for p in range(2):
                sp.wait_ge(o0_stored[p], 16 * NB // 2)
            for r in range(NIN):
                sp.wait_ge(b_scattered[r], 16 * NT * E * NCH // NIN)

        @block.tensor
        def _(pe):
            pe.wait_ge(w_loaded, 16 * NW)
            pe.wait_ge(setup_v, 1)
            pe.matmul(p_misc[0:D, 0, 0:D], w_v[:, :], w_oTp[:, :], start=True, stop=True)
            pe.matmul(p_misc[0:D, 1, 0:E], c_centre[:, :], w_g[:, :], start=True, stop=True)
            pe.matmul(p_sm[0:D, 0, 0:1], w_oTp[:, :], w_bv[:, :], start=True, stop=True)\
                .then_inc(setup_p, 1)
            pe.wait_ge(setup_v, 2)
            pe.matmul(p_st[0:KA, 0, 0:CG], w_bl[:, :], w_cg[:, :], start=True, stop=True)
            pe.matmul(p_st[:, 1, 0:CG], w_lj[:, :], w_cg[:, :], start=True, stop=True)\
                .then_inc(setup_p, 1)
            pe.matmul(p_u[0:KTOK, 0, 0:2 * D], w_e[:, :], w_qk[:, :], start=True, stop=True)
            pe.wait_ge(setup_v, 3)
            pe.matmul(p_u[0:KTOK, 1, 0:GP], w_e[:, :], w_all[:, :], start=True, stop=True)\
                .then_inc(setup_p, 1)
            pe.wait_ge(setup_v, 4)

            def qk_product(n, p):
                pe.wait_ge(xl_ready, n + 1)
                if isinstance(n, int) and n == 1:
                    pe.wait_ge(lo_ready, 1)
                after(pe, v_ready, 2 * n - 2)
                for w, part in ((w_qkh, xh), (w_qkh, xl), (w_qkl, xh)):
                    for a in range(2):
                        last = pe.matmul(p_misc[:, a, :], w[:, :], part[0:KTOK, a * HALF:(a + 1) * HALF],
                                         start=(w is w_qkh and part is xh), stop=(w is w_qkl))
                last.then_inc(qk_done, 1)

            def project(n, p, r, qk_next):
                if r == 0:
                    pe.wait_ge(x_loaded[p], of_parity(n, p, 16))
                    if qk_next:
                        pe.wait_ge(lo_ready, n + 2)
                    after(pe, t_ready, n - 1)
                else:
                    pe.wait_ge(v_ready, 2 * n + 1)
                for j in range(4):
                    t = 4 * r + j
                    last = pe.matmul(p_misc[:, j // 2, (j % 2) * GP:(j % 2 + 1) * GP],
                                     xt[0:KTOK, p, t * P:(t + 1) * P], w_px[:, :], start=True, stop=True)
                last.then_inc(v_done, 1)

            def max_scores(n, p, j):
                if j == 0:
                    pe.wait_ge(spread[p], of_parity(n, p, 96))
                    after(pe, shift_ready, n)
                    after(pe, pos_read, n - 2)
                after(pe, max_done, j - 1 if isinstance(n, int) and n == 0 else NT * n + j)
                for a in range(2):
                    last = pe.matmul(max_place(n, j)[:, a, :], mQ[p][:, j * P:(j + 1) * P],
                                     sK[p][:, a * HALF:(a + 1) * HALF], start=True, stop=True)
                last.then_inc(sm_done, 1)

            def max_turn(n, p):
                wait_apart(pe, max_done, NT * n + NT)
                pe.transpose(p_sm[0:NT, 0, 0:P], mx[:, p, :], c_id[:, :]).then_inc(mt_done, 1)

            def scores(n, p, k):
                if k == 0:
                    pe.wait_ge(shift_ready, n + 1)
                after(pe, exp_done, NT * n + k)
                for a in range(2):
                    pe.matmul(p_st[:, a, :], sK[p][:, k * P:(k + 1) * P],
                              mQ[p][:, a * HALF:(a + 1) * HALF], start=True, stop=False)
                for a in range(2):
                    last = pe.matmul(p_st[:, a, :], sR[p][0:D + NT, k * P:(k + 1) * P],
                                     mR[p][0:D + NT, a * HALF:(a + 1) * HALF], start=False, stop=True)
                last.then_inc(st_done, 1)

            def weighted_sum(n, p, r, halves=(0, 1)):
                if r == 0:
                    pe.wait_ge(v_ready, 2 * n + 2)
                    after(pe, u_ready, n)
                pe.wait_ge(exp_done, NT * n + 2 * r + 2)
                for a in halves:
                    for k in (2 * r, 2 * r + 1):
                        c = D * (k % 2)
                        last = pe.matmul(p_u[c:c + D, a, :], vv[:, p, k, :],
                                         pT[k % 4][:, a * HALF:(a + 1) * HALF],
                                         start=(r == 0), stop=(r == 3))
                if 1 in halves:
                    last.then_inc(pv_done, 1)

            def turn_sums(n, qk_next):
                pe.wait_ge(u_ready, n + 1)
                if qk_next:
                    pe.wait_ge(lo_ready, n + 4)
                else:
                    after(pe, v_ready, 2 * min(n + 2, NB))
                for j in range(NT):
                    last = pe.matmul(p_misc[:, j // 4, (j % 4) * GT:(j % 4 + 1) * GT],
                                     uu[:, j * P:(j + 1) * P], w_j[:, :], start=True, stop=True)
                last.then_inc(turn_done, 1)

            def positions(n):
                pe.wait_ge(oh_ready, n + 1)
                after(pe, tail_g, GS * n)
                pe.wait_ge(max_done, NT * min(n + 3, NB) if isinstance(n, int) else NT * n + 3 * NT)
                pe.matmul(p_pos, ones16[:, :], per_column(acc[:, :], E), start=True, stop=False)
                for j in range(NT):
                    pe.matmul(p_pos[:, j:NT, :], id16[:, :],
                              oh[:, j, :].unsqueeze(1).broadcast_to([P, NT - j, E]),
                              start=False, stop=False, skip_group_check=j > 0)
                pe.matmul(p_pos, strict16[:, :], per_column(ohs[:, :], E), start=False, stop=True)\
                    .then_inc(pos_done, 1)

            def step(b, par, has):
                q = 1 - par
                if has(0):
                    max_turn(b, par)
                if has(-2):
                    positions(b - 2)
                if has(2):
                    qk_product(b + 2, par)
                for k in range(NT):
                    if has(0):
                        scores(b, par, k)
                    if has(-1):
                        if k == 0:
                            weighted_sum(b - 1, q, 3)
                        if k == 1:
                            turn_sums(b - 1, has(2))
                    if k == 2 and has(0):
                        weighted_sum(b, par, 0, (0,))
                    if has(1):
                        max_scores(b + 1, q, k)
                        if k in (3, 6):
                            project(b + 1, q, k // 6, has(2))
                    if has(0):
                        if k == 2:
                            weighted_sum(b, par, 0, (1,))
                        if k in (4, 5):
                            weighted_sum(b, par, 1, (k - 4,))
                        if k == 7:
                            weighted_sum(b, par, 2)
            run_windows(pe, step)

            def rows_turn(i, m):
                c, r = 2 * NCH * i + m, m % NIN
                wait_apart(pe, c_loaded[r], chunk_in(i, m))
                wait_apart(pe, b_xT_ready, c)
                for j in range(NT):
                    last = pe.transpose(p_st[0:D, j // 4, (j % 4) * P:(j % 4 + 1) * P],
                                        b_in[:, r, j, 0:D], c_id[:, :])
                last.then_inc(b_t_done, 1)

            def hidden(c, q):
                pe.wait_ge(b_xT_ready, c + 1)
                for f in range(HB):
                    after(pe, b_relu, HB * c - HB + f + 1)
                    for a in range(2):
                        last = pe.matmul((p_sm, p_u)[f][:, a, :], b_w1[:, q, f * P:(f + 1) * P],
                                         b_xT[0:KA, a * HALF:(a + 1) * HALF], start=True, stop=True)
                    last.then_inc(b_h_done, 1)

            def pair(i, first, last):
                for m in range(2 * NCH):
                    c, q = 2 * NCH * i + m, m // NCH
                    if m % NCH == 0:
                        pe.wait_ge(e_loaded[q], 48 * (i + 1))
                    hidden(c, q)
                    if not (last and m == 2 * NCH - 1):
                        rows_turn(i, m + 1)
                    pe.wait_ge(b_relu, HB * c + HB)
                    after(pe, b_y_read, c - 1)
                    for j in range(NT):
                        for f in range(HB):
                            mm = pe.matmul(p_y[m % 2][:, j, :], b_h[:, f, j * P:(j + 1) * P],
                                           b_w2[:, q, f, :], start=(f == 0), stop=(f == HB - 1))
                    mm.then_inc(b_y_done, 1)
            def keep_warm(n):
                for a in range(n):
                    pe.matmul(p_u[:, a % 2, :], c_id[:, :], pT[0][:, 0:HALF], start=True, stop=True)

            pe.wait_ge(tail_g, GS * NB)
            keep_warm(12)
            rows_turn(0, 0)
            keep_warm(1)
            run_pairs(pe, pair)

        @block.scalar
        def _(act):
            act.wait_ge(const_set, 1)
            act.wait_ge(w_loaded, 16 * NW)
            act.wait_ge(x_loaded[0], 16)
            act.activation(xh[0:KTOK, :], xt[0:KTOK, 0, :], ACT.Copy).then_inc(xh_ready, 1)
            act.wait_ge(setup_v, 4)

            def qk_high(n, p):
                act.wait_ge(qk_done, n + 1)
                if not isinstance(n, int) or n >= 2:
                    act.wait_ge(spread[p], of_parity(n - 2, p, 96))
                act.activation(hi[p][:, :], flat(p_misc), ACT.Copy).then_inc(hi_ready, 1)

            def split_high(n):
                act.wait_ge(raw_loaded, 16 * n)
                act.wait_ge(qk_done, n)
                act.activation(xh[D:KTOK, :], xr[D:KTOK, :], ACT.Copy).then_inc(xh_ready, 1)

            def v_copy(n, p, r):
                act.wait_ge(v_done, 2 * n + r + 1)
                if r == 0:
                    after(act, pv_done, 4 * n - 4)
                    after(act, uc_ready, n - 1)
                pv = p_misc[:, :, 0:2 * GP].rearrange("p a (t c) -> p a t c", c=GP)
                t = slice(4 * r, 4 * r + 4)
                act.activation(vv[:, p, t, 0:D - 1].rearrange("p (a t) c -> p a t c", a=2),
                               pv[:, :, :, 0:D - 1], ACT.Copy)
                act.activation(hh[:, p, t, :].rearrange("p (a t) c -> p a t c", a=2),
                               pv[:, :, :, D - 1:GP], ACT.Copy).then_inc(v_ready, 1)

            def exponent(n, k):
                act.wait_ge(st_done, NT * n + k + 1)
                after(act, pv_done, 4 * n + k // 2 - 1)
                act.activation(pT[k % 4][:, :], flat(p_st), ACT.Exp).then_inc(exp_done, 1)

            def u_copy(n):
                act.wait_ge(pv_done, 4 * n + 4)
                after(act, turn_done, n)
                act.activation(uu[:, :], flat(p_u), ACT.Copy).then_inc(u_ready, 1)

            def square(n):
                act.wait_ge(uc_ready, n + 1)
                after(act, vs_ready, n)
                act.activation(sq[:, :, :], uc[:, :, 0:D], ACT.Square).then_inc(sq_ready, 1)

            def gate_exp(n):
                act.wait_ge(gap_ready, n + 1)
                after(act, prob_ready, n)
                act.activation(ex[:, :, :], ld[:, :, :], ACT.Exp).then_inc(ex_ready, 1)

            def step(b, par, has):
                q = 1 - par
                if has(2):
                    qk_high(b + 2, par)
                for k in range(NT):
                    if k == 1 and has(-1):
                        u_copy(b - 1)
                    if k == 1 and has(3):
                        split_high(b + 3)
                    if has(0):
                        exponent(b, k)
                    if k == 3 and has(-1):
                        square(b - 1)
                    if k == 7 and has(-1):
                        gate_exp(b - 1)
                    if k in (3, 6) and has(1):
                        v_copy(b + 1, q, k // 6)
            run_windows(act, step)

            def xT_copy(c):
                act.wait_ge(b_t_done, c + 1)
                after(act, b_h_done, HB * c)
                act.activation(b_xT[0:D, :], flat(p_st)[0:D, :], ACT.Copy).then_inc(b_xT_ready, 1)

            def squares(c):
                act.wait_ge(b_c_ready, c + 1)
                act.activation(b_sq[:, :, :], b_c[:, :, :], ACT.Square).then_inc(b_sq_ready, 1)

            def deviation(c):
                act.wait_ge(b_vs_ready, c + 1)
                act.activation(b_sd[:, :], b_vs[:, :], ACT.Sqrt, bias=b_eps[:, 0:1], scale=1.0 / D)\
                    .then_inc(b_sd_ready, 1)

            def pair(i, first, last):
                for m in range(2 * NCH):
                    c = 2 * NCH * i + m
                    after(act, b_y_done, c)
                    for f in range(HB):
                        act.wait_ge(b_h_done, HB * c + f + 1)
                        act.activation(b_h[:, f, :], flat((p_sm, p_u)[f]), ACT.Relu)\
                            .then_inc(b_relu, 1)
                    lag = 1 if first and m < 3 else 2
                    if first and m < 3:
                        xT_copy(c + 1)
                    if not (first and m in (0, 3)):
                        squares(c - lag)
                    if not (first and m < 3 or last and m == 2 * NCH - 1):
                        xT_copy(c + 1)
                    if not (first and m in (0, 3)):
                        deviation(c - lag)
            act.wait_ge(pool_set, POOL_SET)
            xT_copy(0)
            run_pairs(act, pair)
            for c in range(E * NCH - 2, E * NCH):
                squares(c)
                deviation(c)

        @block.vector
        def _(dve):
            links = [1]

            def link(ins):
                links[0] += 1
                ins.then_inc(set_link, 1)
                dve.wait_ge(set_link, links[0])

            dve.memset(xt[D:KA, :, :], 1.0)
            dve.memset(xr[D:KA, :], 1.0)
            dve.memset(w_all[:, :], 0.0)
            dve.memset(w_e[D:KA, :], 0.0).then_inc(set_link, 1)
            dve.wait_ge(set_link, 1)
            dve.memset(w_e[D:KA, D:KA], 1.0).then_inc(const_set, 1)
            dve.wait_ge(const_set, 1)
            dve.wait_ge(w_loaded, 16 * NW)
            dve.tensor_scalar(w_oTp[:, :], w_oT[:, :], w_oT[:, D - 1:D], None, ALU.subtract)\
                .then_inc(setup_v, 1)
            dve.tensor_copy(w_e[0:D, :], w_t[:, :])
            dve.tensor_copy(w_all[:, GP - 2:GP - 1], w_qk[:, 0:1])
            dve.tensor_copy(w_all[:, GP - 1:GP], w_qk[:, D:D + 1])
            dve.tensor_copy(w_j[:, GT - 1:GT], c_sum[:, :])
            dve.tensor_copy(w_cg[:, 0:D], c_centre[:, :])
            dve.tensor_copy(w_lj[:, 0:D], c_id[0:D, 0:D])
            link(dve.tensor_copy(w_lj[:, D:P], c_id[0:D, 0:D]))
            dve.wait_ge(setup_p, 1)
            dve.tensor_copy(w_all[0:D, 0:D - 1], p_misc[0:D, 0, 0:D - 1])
            dve.tensor_copy(w_cg[:, D:CG], p_misc[0:D, 1, 0:E])
            dve.tensor_copy(w_lj[:, D - 1:D], p_sm[0:D, 0, 0:1])
            dve.tensor_copy(w_lj[:, P - 1:P], p_sm[0:D, 0, 0:1]).then_inc(setup_v, 1)
            dve.wait_ge(setup_p, 2)
            dve.tensor_copy(w_all[:, D - 1:D - 1 + CG], p_st[0:KA, 0, 0:CG])
            dve.tensor_copy(w_j[:, 0:CG], p_st[:, 1, 0:CG]).then_inc(setup_v, 1)
            dve.wait_ge(setup_p, 3)
            dve.tensor_scalar(w_qkx[:, 0:D], p_u[0:KTOK, 0, 0:D], D ** -0.5, None, ALU.mult)
            link(dve.tensor_copy(w_qkx[:, D:2 * D], p_u[0:KTOK, 0, D:2 * D]))
            link(dve.tensor_copy(w_qkh[:, :], w_qkx[:, :]))
            dve.tensor_tensor(w_qkl[:, :], w_qkx[:, :], w_qkh[:, :].bitcast(F32), ALU.subtract)
            dve.tensor_copy(w_px[:, :], p_u[0:KTOK, 1, 0:GP]).then_inc(setup_v, 1)

            dve.wait_ge(xh_ready, 1)
            dve.tensor_tensor(xl[0:KTOK, :], xt[0:KTOK, 0, :], xh[0:KTOK, :].bitcast(F32), ALU.subtract)\
                .then_inc(xl_ready, 1)

            dve.tensor_copy(id16[:, :], c_id[:, :])
            dve.tensor_copy(strict16[:, :], c_strict[:, :])
            dve.tensor_scalar(c_neg[:, :], c_id[0:E, 0:E], -1.0, None, ALU.mult)
            dve.memset(b_xT[D:KA, :], 1.0)
            dve.memset(vv[:, :, :, D - 1:D], 1.0)
            for p in range(2):
                dve.memset(sR[p][D:D + NT, :].bitcast(F32), 1.0)
            dve.memset(ones16[:, :], 1.0)
            dve.memset(c_half[:, :], -0.5)
            dve.memset(b_eps[:, :], EPS)
            dve.memset(b_big[:, 0, :], 1e4)
            dve.memset(b_big[:, 1, :], -1e4)
            dve.memset(b_big[:, 2, :], 0.0)
            dve.memset(acc[:, :], 0.0).then_inc(const_set, 1)

            def split_low(n):
                dve.wait_ge(xh_ready, n + 1)
                dve.wait_ge(qk_done, n)
                dve.tensor_tensor(xl[D:KTOK, :], xr[D:KTOK, :], xh[D:KTOK, :].bitcast(F32), ALU.subtract)\
                    .then_inc(xl_ready, 1)

            def qk_low(n, p):
                dve.wait_ge(hi_ready, n + 1)
                if not isinstance(n, int) or n >= 2:
                    dve.wait_ge(spread[p], of_parity(n - 2, p, 96))
                dve.tensor_tensor(lo[p][:, :], flat(p_misc), hi[p][:, :].bitcast(F32), ALU.subtract)\
                    .then_inc(lo_ready, 1)

            def row_max(n, p, j):
                dve.wait_ge(sm_done, NT * n + j + 1)
                if j == 0:
                    after(dve, mt_done, n - 1)
                dve.tensor_reduce(mx[:, p, j:j + 1], flat(max_place(n, j)), AX.X, ALU.max).then_inc(max_done, 1)

            def shift(n, p):
                dve.wait_ge(mt_done, n + 1)
                after(dve, st_done, NT * n - NT)
                dve.tensor_tensor(
                    mR[p][D:D + NT, :].rearrange("p (b c) -> p b c", c=P),
                    p_sm[0:NT, 0, 0:P].unsqueeze(1).broadcast_to([NT, NT, P]),
                    c_neg[:, :].unsqueeze(2).broadcast_to([NT, NT, P]), ALU.mult).then_inc(shift_ready, 1)

            TS = 3

            def attend(n, p):
                def step(i, ins):
                    ins.then_inc(tail_v, 1)
                    dve.wait_ge(tail_v, TS * n + i)

                dve.wait_ge(turn_done, n + 1)
                dve.wait_ge(v_ready, 2 * n + 2)
                after(dve, uc_ready, n)
                dve.reciprocal(rs[:, :].rearrange("p (a t) -> p a t", a=2), turned[:, :, :, GT - 1])
                step(1, dve.tensor_scalar(kz[:, :], hh[:, p, :, GH - 1], 0.0, None, ALU.not_equal))
                step(2, dve.scalar_tensor_tensor(out=mk[:, :], in0=hh[:, p, :, GH - 2], scalar=0.0,
                                                 in1=kz[:, :], op0=ALU.not_equal, op1=ALU.mult))
                step(3, dve.tensor_tensor(rm[:, :], rs[:, :], mk[:, :], ALU.mult))
                dve.tensor_tensor(four(tt[:, :, :]), turned[:, :, :, 0:CG],
                                  four(per_token(rm[:, :], CG)), ALU.mult).then_inc(t_ready, 1)

            def sum_squares(n):
                dve.wait_ge(sq_ready, n + 1)
                after(dve, rstd_ready, n)
                dve.tensor_reduce(vs[:, :], sq[:, :, :], AX.X, ALU.add).then_inc(vs_ready, 1)

            def gate_step(n, i, ins):
                ins.then_inc(tail_g, 1)
                dve.wait_ge(tail_g, GS * n + i)

            def gate_logits(n):
                dve.wait_ge(rstd_ready, n + 1)
                gate_step(n, 1, dve.tensor_tensor(lg[:, :, :], uc[:, :, D:CG],
                                                  per_token(rstd[:, :], E), ALU.mult))
                gate_step(n, 2, dve.tensor_tensor(lb[:, :, :], lg[:, :, :],
                                                  per_column(c_gb[:, :], E), ALU.add))
                gate_step(n, 3, dve.tensor_reduce(lm[:, :], lb[:, :, :], AX.X, ALU.max))

            def gate_gaps(n):
                after(dve, ex_ready, n)
                dve.tensor_tensor(ld[:, :, :], lb[:, :, :], per_token(lm[:, :], E), ALU.subtract)\
                    .then_inc(gap_ready, 1)
                dve.wait_ge(gap_ready, n + 1)
                gate_step(n, 4, dve.scalar_tensor_tensor(
                    out=pri[:, :, :], in0=ld[:, :, :], scalar=0.0, in1=per_column(c_desc[:, :], E),
                    op0=ALU.is_equal, op1=ALU.mult))
                gate_step(n, 5, dve.tensor_reduce(pm[:, :], pri[:, :, :], AX.X, ALU.max))

            def gate_choice(n):
                gate_step(n, 6, dve.tensor_tensor(oh[:, :, :], pri[:, :, :], per_token(pm[:, :], E),
                                                  ALU.is_equal))
                with nc.allow_low_precision("counts up to 8"):
                    dve.tensor_reduce(ohs[:, :], oh[:, :, :].rearrange("p j e -> p e j"), AX.X, ALU.add)\
                        .then_inc(oh_ready, 1)

            def probability(n, p):
                dve.wait_ge(ex_ready, n + 1)
                gate_step(n, 7, dve.tensor_reduce(se[:, :], ex[:, :, :], AX.X, ALU.add))
                after(dve, scattered[p], of_parity(n - 2, p, 16 * NT) if not isinstance(n, int) or n >= 2
                      else 0)
                dve.reciprocal(rows[:, p, :, D], se[:, :]).then_inc(prob_ready, 1)

            def slot_index(n, p):
                dve.wait_ge(pos_done, n + 1)
                gate_step(n, 8, dve.tensor_scalar(far[:, :, :], p_pos, float(CAP), FAR,
                                                  ALU.is_gt, ALU.mult))
                dve.tensor_tensor(pa[:, :, :], p_pos, far[:, :, :], ALU.add).then_inc(pos_read, 1)
                dve.wait_ge(pos_read, n + 1)
                gate_step(n, 9, dve.tensor_tensor(pb[:, :, :], pa[:, :, :],
                                                  per_column(c_slot0[:, :], E), ALU.add))
                gate_step(n, 10, dve.tensor_tensor(pc[:, :, :], pb[:, :, :], oh[:, :, :], ALU.mult))
                gate_step(n, 11, dve.tensor_reduce(si[:, :], pc[:, :, :], AX.X, ALU.add))
                gate_step(n, 12, dve.tensor_copy(idx[:, p, :], si[:, :]))
                with nc.allow_low_precision("counts up to 256"):
                    gate_step(n, 13, dve.tensor_tensor(acc[:, :], acc[:, :], ohs[:, :], ALU.add))

            def step(b, par, has):
                q = 1 - par
                if has(0):
                    shift(b, par)
                if has(-2):
                    probability(b - 2, par)
                    slot_index(b - 2, par)
                if has(2):
                    qk_low(b + 2, par)
                for j in range(NT):
                    if has(1):
                        row_max(b + 1, q, j)
                    if j == 0 and has(3):
                        split_low(b + 3)
                    if has(-1):
                        if j == 1:
                            attend(b - 1, q)
                        if j == 3:
                            sum_squares(b - 1)
                        if j == 5:
                            gate_logits(b - 1)
                        if j == 6:
                            gate_gaps(b - 1)
                        if j == 7:
                            gate_choice(b - 1)
            run_windows(dve, step)

            BS = 10
            BP = 4

            def expert_out(i, m):
                q = m // NCH % 2
                wait_apart(dve, b_y_done, 2 * NCH * i + m + 1)
                wait_apart(dve, e_loaded[q], 48 * (i + m // (2 * NCH)) + 48)
                dve.tensor_tensor(b_y[:, m % 2, :, :], p_y[m % 2], per_column(b_b2[:, q, :], D), ALU.add)\
                    .then_inc(b_y_read, 1)

            def chunk(i, m, start, end, base):
                c = 2 * NCH * i + m
                y, ny = b_y[:, m % 2, :, :], b_y[:, (m + 1) % 2, :, :]
                r = m % NIN
                done = [base]

                def count(ins):
                    done[0] = done[0] + 1
                    ins.then_inc(b_tail, 1)
                    return done[0]

                def replace(k, since):
                    wait_apart(dve, b_tail, since)
                    return count(dve.copy_predicated(ny, b_m[:, k, :, :], per_column(b_big[:, k, :], D)))

                if not start:
                    wait_apart(dve, b_tail, base)
                    wait_apart(dve, c_loaded[r], chunk_in(i, m))
                    p_at = count(dve.tensor_tensor(b_p[:, :, :], y, per_token(b_in[:, r, :, D], D), ALU.mult))
                if not end:
                    expert_out(i, m + 1)
                if not start:
                    wait_apart(dve, b_tail, p_at)
                    u_at = count(dve.tensor_tensor(b_u[:, :, :], b_p[:, :, :], b_in[:, r, :, 0:D], ALU.add))
                if not end:
                    dve.wait_ge(b_y_read, c + 2)
                    dve.tensor_scalar(b_m[:, 0, :, :], ny, FMAX, None, ALU.is_gt)
                    dve.tensor_scalar(b_m[:, 1, :, :], ny, -FMAX, None, ALU.is_lt)
                if not start:
                    wait_apart(dve, b_tail, u_at)
                    mu_at = count(dve.tensor_reduce(b_mu[:, :], b_u[:, :, :], AX.X, ALU.add))
                if not end:
                    masks_at = count(dve.tensor_tensor(b_m[:, 2, :, :], ny, ny, ALU.not_equal))
                if not start:
                    wait_apart(dve, b_tail, mu_at)
                    mm_at = count(dve.tensor_scalar(b_mm[:, :], b_mu[:, :], 1.0 / D, None, ALU.mult))
                if not end:
                    one_at = replace(0, masks_at)
                if not start:
                    wait_apart(dve, b_tail, mm_at)
                    dve.tensor_tensor(b_c[:, :, :], b_u[:, :, :], per_token(b_mm[:, :], D), ALU.subtract)\
                        .then_inc(b_c_ready, 1)
                if not end:
                    two_at = replace(1, one_at)
                if not start:
                    if not (isinstance(i, int) and i == 0 and m < NIN):
                        wait_apart(dve, b_scattered[r], 16 * NT * ((2 * NCH // NIN) * i + m // NIN))
                    count(dve.tensor_copy(b_ix[:, r, :], b_in[:, r, :, D + 1]))
                    dve.wait_ge(b_sq_ready, c + 1)
                    dve.tensor_reduce(b_vs[:, :], b_sq[:, :, :], AX.X, ALU.add).then_inc(b_vs_ready, 1)
                if not end:
                    replace(2, two_at)
                if not start:
                    dve.wait_ge(b_sd_ready, c + 1)
                    rs_at = count(dve.reciprocal(b_rs[:, :], b_sd[:, :]))
                    wait_apart(dve, b_tail, rs_at)
                    dve.tensor_tensor(b_o[:, r, :, :], b_c[:, :, :], per_token(b_rs[:, :], D), ALU.mult)\
                        .then_inc(b_o_ready, 1)

            chunk(0, -1, True, False, 0)

            def pair(i, first, last):
                for m in range(2 * NCH):
                    base = BP + BS * (2 * NCH * i + m)
                    if first and m < 2:
                        chunk(i, m, False, True, base)
                        chunk(i, m, True, False, base + BS - BP)
                    else:
                        chunk(i, m, False, last and m == 2 * NCH - 1, base)
            run_pairs(dve, pair)

        @block.gpsimd
        def _(pool):
            pool.memset(init[:, :, :], 0.0).then_inc(pool_set, 1)
            pool.wait_ge(pool_set, 1)
            pool.memset(init[:, :, D + 1:ROW], FAR).then_inc(pool_set, 1)
            pool.wait_ge(pool_set, 2)
            for k in range(NINIT):
                if k == 0:
                    pool.wait_ge(x_loaded[1], 16)
                elif k == 5:
                    pool.wait_ge(spread[1], 96)
                elif k == 8:
                    pool.wait_ge(exp_done, 1)
                pool.dma_start(slots_i[k, :, :], init[:, :, :].rearrange("p a w -> p (a w)"))\
                    .then_inc(init_stored, 16)
            pool.wait_ge(w_loaded, 16 * NW)
            pool.wait_ge(const_set, 2)
            pool.wait_ge(init_stored, 16 * NINIT)

            PS = 7

            def residual(n, p):
                wait_apart(pool, t_ready, n + 1)
                wait_apart(pool, v_ready, 2 * n + 2)
                wait_apart(pool, oh_ready, n)
                wait_apart(pool, sq_ready, n)
                pool.tensor_tensor(uc[:, :, :], tt[:, :, :], hh[:, p, :, 0:CG], ALU.add)\
                    .then_inc(uc_ready, 1)

            def counted(n, i, ins):
                ins.then_inc(pool_step, 1)
                wait_apart(pool, pool_step, PS * n + i)

            def normalize(n, p):
                wait_apart(pool, vs_ready, n + 1)
                counted(n, 1, pool.tensor_scalar(ve[:, 0, :], vs[:, :], 1.0 / D, EPS, ALU.mult, ALU.add))
                pool.tensor_tensor(rstd[:, :], ve[:, 0, :], c_half[:, :], ALU.pow).then_inc(rstd_ready, 1)
                counted(n, 2, pool.tensor_scalar(vr[:, :], vs[:, :], 1.0 / D, None, ALU.mult))
                if not isinstance(n, int) or n >= 2:
                    pool.wait_ge(scattered[p], of_parity(n - 2, p, 16 * NT))
                pool.tensor_tensor(rows[:, p, :, 0:D], uc[:, :, 0:D], per_token(rstd[:, :], D), ALU.mult)
                counted(n, 3, pool.tensor_copy(rows[:, p, :, D + 1], c_tok[:, :]))

            def default_rows(n, p):
                counted(n, 4, pool.tensor_scalar(ve[:, 1, :], ve[:, 0, :], EPS, None, ALU.mult))
                counted(n, 5, pool.tensor_tensor(ve[:, 1, :], ve[:, 1, :], vr[:, :], ALU.add))
                counted(n, 6, pool.tensor_tensor(rst2[:, :], ve[:, 1, :], c_half[:, :], ALU.pow))
                if not isinstance(n, int) or n >= 2:
                    wait_apart(pool, o0_stored[p], of_parity(n - 2, p, 16))
                pool.tensor_tensor(o0[:, p, :, :], uc[:, :, 0:D], per_token(rst2[:, :], D), ALU.mult)\
                    .then_inc(o0_ready, 1)
                counted(n, 7, pool.tensor_scalar(c_tok[:, :], c_tok[:, :], float(S), None, ALU.add))

            def scatter(n, p, tiles):
                if 0 in tiles:
                    wait_apart(pool, prob_ready, n + 1)
                    wait_apart(pool, tail_g, GS * n + GS)
                    wait_apart(pool, pool_step, PS * n + 3)
                for j in tiles:
                    pool.indirect_dma_start(slots, bass.IndirectOffsetOnAxis(ap=idx[:, p, j:j + 1], axis=0),
                                            rows[:, p, j, :], None, bounds_check=SLOTS - 1,
                                            oob_is_err=False).then_inc(scattered[p], 16)

            def step(b, par, has):
                full = has(0)
                if has(-2):
                    scatter(b - 2, par, range(6 if full else 4))
                if has(-1):
                    residual(b - 1, 1 - par)
                if has(-2):
                    scatter(b - 2, par, range(6, NT) if full else range(4, 6))
                if has(-1):
                    normalize(b - 1, 1 - par)
                if has(-2) and not full:
                    scatter(b - 2, par, range(6, NT))
                if has(-1) and full:
                    default_rows(b - 1, 1 - par)
                elif has(-2) and not has(-1):
                    default_rows(b - 2, par)
            run_windows(pool, step)

            for p in range(2):
                pool.wait_ge(o0_stored[p], 16 * NB // 2)

            def pair(i, first, last):
                for m in range(2 * NCH):
                    wait_apart(pool, b_o_ready, 2 * NCH * i + m + 1)
                    for j in range(NT):
                        pool.indirect_dma_start(out_rows, bass.IndirectOffsetOnAxis(
                            ap=b_ix[:, m % NIN, j:j + 1], axis=0), b_o[:, m % NIN, j, :], None,
                            bounds_check=T - 1, oob_is_err=False).then_inc(b_scattered[m % NIN], 16)
            run_pairs(pool, pair)


_INS = ["x", "posT", "wqk", "wide", "deep", "w1", "w2", "b2"]


def kernel(x, L0_tok_W, L0_tok_b, L0_tok_pos, L0_attn_Wq, L0_attn_bq, L0_attn_Wk, L0_attn_bk, L0_attn_Wv,
           L0_attn_bv, L0_attn_Wo, L0_attn_bo, L0_ffn_gate_w, L0_ffn_gate_b, L0_ffn_w1, L0_ffn_b1,
           L0_ffn_w2, L0_ffn_b2):
    import concourse.bacc as bacc
    from concourse.bass_utils import run_bass_kernel_spmd

    n = 32
    f = np.float32

    def columns(a):
        return a.reshape(*a.shape[:-1], P, NT).swapaxes(-1, -2).reshape(a.shape)

    patches = np.asarray(x).reshape(NB, n, 7, n, 7).transpose(0, 2, 4, 1, 3).reshape(NB, PATCH, S)
    wq, wk = np.asarray(L0_attn_Wq), np.asarray(L0_attn_Wk)
    up = np.concatenate([np.asarray(L0_ffn_w1), np.asarray(L0_ffn_b1)[:, None, :]], axis=1)
    down = np.asarray(L0_ffn_w2).reshape(E, HB, P, D).transpose(0, 2, 1, 3)
    sumcol = np.zeros((P, 1), f)
    sumcol[[D - 1, P - 1]] = 1
    arrays = {
        "x": columns(patches),
        "posT": columns(np.asarray(L0_tok_pos)[0].T),
        "wqk": np.concatenate([np.concatenate([wq.T, wk.T], axis=1),
                               np.concatenate([np.asarray(L0_attn_bq), np.asarray(L0_attn_bk)])[None]]),
        "w1": up,
        "w2": down,
        "b2": np.broadcast_to(np.asarray(L0_ffn_b2)[:, None, :], (E, P, D)),
        "wide": np.concatenate([
            np.eye(P, dtype=f), np.triu(np.ones((P, P), f), 1), sumcol,
            np.broadcast_to(np.arange(E, 0, -1, dtype=f), (P, E)),
            np.broadcast_to(np.arange(E, dtype=f) * CAP - 1, (P, E)),
            np.arange(S, dtype=f).reshape(P, NT),
            np.broadcast_to(np.asarray(L0_ffn_gate_b), (P, E))], axis=1),
        "deep": np.concatenate([
            np.eye(D, dtype=f), np.asarray(L0_tok_b)[:, None], np.asarray(L0_tok_W),
            np.eye(D, dtype=f) - f(1 / D), np.asarray(L0_attn_Wv), np.asarray(L0_attn_Wo).T,
            np.asarray(L0_ffn_gate_w), np.asarray(L0_attn_bv)[:, None],
            np.eye(D, dtype=f), np.asarray(L0_attn_bo)[:, None]], axis=1),
    }
    nc = bacc.Bacc("TRN2", target_bir_lowering=False, num_devices=1)
    args, given = [], {}
    for name in _INS:
        a = np.ascontiguousarray(arrays[name])
        given[f"in_{name}"] = a
        args.append(nc.dram_tensor(f"in_{name}", a.shape, mybir.dt.from_np(a.dtype), kind="ExternalInput").ap())
    out = nc.dram_tensor("out_0", (NB, S, D), F32, kind="ExternalOutput").ap()
    build(nc, *args, out)
    r = run_bass_kernel_spmd(nc, [given], core_ids=[0])
    return r.results[0]["out_0"]
```
